# Optimizing a Trainium2 kernel written in Bass

```python
import numpy as np
import jax
import jax.numpy as jnp

def _softmax(x, axis=-1):
    return jax.nn.softmax(x, axis=axis)

def _gelu(x):
    return jax.nn.gelu(x, approximate=True)

def _silu(x):
    return jax.nn.silu(x)

def _sigmoid(x):
    return jax.nn.sigmoid(x)

def _layernorm(x, axis=-1, eps=1e-05):
    m = jnp.mean(x, axis=axis, keepdims=True)
    v = jnp.var(x, axis=axis, keepdims=True)
    return (x - m) / jnp.sqrt(v + eps)

def _scatter_add(tgt, idx, src, axis=0):
    return tgt.at[idx].add(src)

def _segment_sum(src, seg, n):
    return jax.ops.segment_sum(src, seg, n)
kernel_name = 'mk_adj_resnorm_d4_adj_r2_b6f638'

def setup_inputs(seed: int=0):
    np.random.seed(seed)
    _w = jnp.asarray

    def _rec_inputs():
        import jax
        import jax.numpy as jnp
        _gk = jax.random.key(seed)
        x = -0.0003929 + 0.9999 * jax.random.normal(jax.random.fold_in(_gk, 1), (32, 256, 512), jnp.float32)
        _w = (1.0 + jnp.arange(256, dtype=jnp.float32)) ** (-0.5)
        _w = _w / _w.mean()
        _pij = jnp.clip(0.0078125 * _w[:, None] * _w[None, :], 0.0, 1.0)
        _a = jax.random.uniform(jax.random.fold_in(_gk, 2), (256, 256)) < _pij
        _a = jnp.logical_or(_a, jnp.swapaxes(_a, -1, -2))
        _a = jnp.logical_or(_a, jnp.eye(256, dtype=bool))
        _af = _a.astype(jnp.float32)
        _af = _af * jax.random.uniform(jax.random.fold_in(_gk, 3), (256, 256), jnp.float32, 0.05, 0.198159)
        adj = _af
        return (x, adj)
    x, adj = _rec_inputs()

    def _L0_gnn_setup():
        import jax, jax.numpy as jnp
        import numpy as np
        NEG_SLOPE = 0.01
        key = jax.random.key(seed)
        k1, k2, k3, k4, k5 = jax.random.split(key, 5)
        B, C, N, O = (32, 256, 512, 256)
        x = jax.random.normal(k1, (B, C, N), dtype=jnp.float32)
        wq = jax.random.normal(k2, (C,), dtype=jnp.float32) * (1.0 / np.sqrt(C))
        wk = jax.random.normal(k3, (C,), dtype=jnp.float32) * (1.0 / np.sqrt(C))
        wm = jax.random.normal(k4, (O, C), dtype=jnp.float32) * (1.0 / np.sqrt(C))
        bm = jax.random.normal(k5, (O,), dtype=jnp.float32) * 0.01
        return {'x': x, 'wq': wq, 'wk': wk, 'wm': wm, 'bm': bm}
    _L0_gnn_all = _L0_gnn_setup()
    _L0_gnn_in = {k: v for k, v in _L0_gnn_all.items() if k in ('wq', 'wk', 'bm')}
    del _L0_gnn_all

    def _L1_gnn_setup():
        import jax, jax.numpy as jnp
        import numpy as np
        DIM = 199
        K_HOP = 3

        def _khop_support(n, k):
            A = np.eye(n, dtype=np.float64)
            idx = np.arange(n)
            A[idx, (idx + 1) % n] = 1.0
            A[(idx + 1) % n, idx] = 1.0
            S = np.linalg.matrix_power(A, k)
            return (S > 0).astype(np.float32)
        key = jax.random.key(seed)
        kx, kk = jax.random.split(key)
        batch, n, f = (128, DIM, 512)
        x = jax.random.normal(kx, (batch, n, f), dtype=jnp.float32)
        support = jnp.asarray(_khop_support(n, K_HOP))
        limit = float(np.sqrt(6.0 / (n + n)))
        kernel = jax.random.uniform(kk, (n, n), minval=-limit, maxval=limit, dtype=jnp.float32)
        bias = jnp.zeros((f,), dtype=jnp.float32)
        return {'x': x, 'support': support, 'kernel': kernel, 'bias': bias}
    _L1_gnn_all = _L1_gnn_setup()
    _L1_gnn_in = {k: v for k, v in _L1_gnn_all.items() if k in ('bias',)}
    del _L1_gnn_all

    def _L2_gnn_setup():
        import jax, jax.numpy as jnp
        import numpy as np
        EPS = 1e-08

        def _row_stochastic_causal(A, causal_mask):
            A = A * causal_mask
            deg = jnp.maximum(A.sum(axis=-1, keepdims=True), EPS)
            return A / deg
        key = jax.random.key(seed)
        k = jax.random.split(key, 5)
        B, N, D = (4, 1024, 512)
        s = 1.0 / np.sqrt(D)
        h = jax.random.normal(k[0], (B, N, D), dtype=jnp.float32)
        W_lang = jax.random.normal(k[1], (D, D), dtype=jnp.float32) * s
        W_grav = jax.random.normal(k[2], (D, D), dtype=jnp.float32) * s
        W_V = jax.random.normal(k[3], (D, D), dtype=jnp.float32) * s
        W_O = jax.random.normal(k[4], (D, D), dtype=jnp.float32) * s
        causal_mask = jnp.tril(jnp.ones((N, N), dtype=jnp.float32))
        gate_logit = jnp.zeros((), jnp.float32)
        log_sigma = jnp.zeros((), jnp.float32)
        return {'h': h, 'causal_mask': causal_mask, 'W_lang': W_lang, 'W_grav': W_grav, 'W_V': W_V, 'W_O': W_O, 'gate_logit': gate_logit, 'log_sigma': log_sigma}
    _L2_gnn_all = _L2_gnn_setup()
    _L2_gnn_in = {k: v for k, v in _L2_gnn_all.items() if k in ('W_lang', 'W_grav', 'W_V', 'W_O', 'gate_logit', 'log_sigma')}
    del _L2_gnn_all

    def _L3_gnn_setup():
        import jax, jax.numpy as jnp
        import numpy as np
        EPS = 1e-08

        def _row_stochastic_causal(A, causal_mask):
            A = A * causal_mask
            deg = jnp.maximum(A.sum(axis=-1, keepdims=True), EPS)
            return A / deg
        key = jax.random.key(seed)
        k = jax.random.split(key, 5)
        B, N, D = (4, 1024, 512)
        s = 1.0 / np.sqrt(D)
        h = jax.random.normal(k[0], (B, N, D), dtype=jnp.float32)
        W_lang = jax.random.normal(k[1], (D, D), dtype=jnp.float32) * s
        W_grav = jax.random.normal(k[2], (D, D), dtype=jnp.float32) * s
        W_V = jax.random.normal(k[3], (D, D), dtype=jnp.float32) * s
        W_O = jax.random.normal(k[4], (D, D), dtype=jnp.float32) * s
        causal_mask = jnp.tril(jnp.ones((N, N), dtype=jnp.float32))
        gate_logit = jnp.zeros((), jnp.float32)
        log_sigma = jnp.zeros((), jnp.float32)
        return {'h': h, 'causal_mask': causal_mask, 'W_lang': W_lang, 'W_grav': W_grav, 'W_V': W_V, 'W_O': W_O, 'gate_logit': gate_logit, 'log_sigma': log_sigma}
    _L3_gnn_all = _L3_gnn_setup()
    _L3_gnn_in = {k: v for k, v in _L3_gnn_all.items() if k in ('W_lang', 'W_grav', 'W_V', 'W_O', 'gate_logit', 'log_sigma')}
    del _L3_gnn_all
    return {'x': x, 'adj': adj, 'L0_gnn_wq': _L0_gnn_in['wq'], 'L0_gnn_wk': _L0_gnn_in['wk'], 'L0_gnn_bm': _L0_gnn_in['bm'], 'L1_gnn_bias': _L1_gnn_in['bias'], 'L2_gnn_W_lang': _L2_gnn_in['W_lang'], 'L2_gnn_W_grav': _L2_gnn_in['W_grav'], 'L2_gnn_W_V': _L2_gnn_in['W_V'], 'L2_gnn_W_O': _L2_gnn_in['W_O'], 'L2_gnn_gate_logit': _L2_gnn_in['gate_logit'], 'L2_gnn_log_sigma': _L2_gnn_in['log_sigma'], 'L3_gnn_W_lang': _L3_gnn_in['W_lang'], 'L3_gnn_W_grav': _L3_gnn_in['W_grav'], 'L3_gnn_W_V': _L3_gnn_in['W_V'], 'L3_gnn_W_O': _L3_gnn_in['W_O'], 'L3_gnn_gate_logit': _L3_gnn_in['gate_logit'], 'L3_gnn_log_sigma': _L3_gnn_in['log_sigma']}

def reference(x, adj, L0_gnn_wq, L0_gnn_wk, L0_gnn_bm, L1_gnn_bias, L2_gnn_W_lang, L2_gnn_W_grav, L2_gnn_W_V, L2_gnn_W_O, L2_gnn_gate_logit, L2_gnn_log_sigma, L3_gnn_W_lang, L3_gnn_W_grav, L3_gnn_W_V, L3_gnn_W_O, L3_gnn_gate_logit, L3_gnn_log_sigma):
    import jax
    import jax.numpy as jnp

    def _L0_gnn_ref(x, wq, wk, wm, bm):
        import jax, jax.numpy as jnp
        import numpy as np
        NEG_SLOPE = 0.01
        q = jnp.einsum('c,bcn->bn', wq, x)
        k = jnp.einsum('c,bcn->bn', wk, x)
        scores = q[:, None, :] + k[:, :, None]
        scores = jnp.where(scores > 0, scores, NEG_SLOPE * scores)
        att = jax.nn.softmax(scores, axis=-1)
        agg = jnp.einsum('bcn,bmn->bcm', x, att)
        out = jnp.einsum('oc,bcm->bom', wm, agg) + bm[None, :, None]
        return jax.nn.relu(out)

    def _L1_gnn_ref(x, support, kernel, bias):
        import jax, jax.numpy as jnp
        import numpy as np
        DIM = 199
        K_HOP = 3

        def _khop_support(n, k):
            A = np.eye(n, dtype=np.float64)
            idx = np.arange(n)
            A[idx, (idx + 1) % n] = 1.0
            A[(idx + 1) % n, idx] = 1.0
            S = np.linalg.matrix_power(A, k)
            return (S > 0).astype(np.float32)
        W = support * kernel
        out = jnp.einsum('bnf,nm->bmf', x, W)
        out = out + bias
        return out

    def _L2_gnn_ref(h, causal_mask, W_lang, W_grav, W_V, W_O, gate_logit, log_sigma):
        import jax, jax.numpy as jnp
        import numpy as np
        EPS = 1e-08

        def _row_stochastic_causal(A, causal_mask):
            A = A * causal_mask
            deg = jnp.maximum(A.sum(axis=-1, keepdims=True), EPS)
            return A / deg
        z_l = jnp.einsum('bnd,ed->bne', h, W_lang)
        z_g = jnp.einsum('bnd,ed->bne', h, W_grav)
        v = jnp.einsum('bnd,ed->bne', h, W_V)
        N = h.shape[-2]
        not_eye = 1.0 - jnp.eye(N, dtype=h.dtype)
        zn = z_l / jnp.maximum(jnp.linalg.norm(z_l, axis=-1, keepdims=True), EPS)
        A_l = jnp.maximum(jnp.einsum('bnd,bmd->bnm', zn, zn), 0.0) * not_eye
        sq = jnp.sum(z_g * z_g, axis=-1, keepdims=True)
        d2 = jnp.maximum(sq + jnp.swapaxes(sq, -1, -2) - 2.0 * jnp.einsum('bnd,bmd->bnm', z_g, z_g), 0.0)
        sigma = jnp.exp(log_sigma)
        A_g = jnp.exp(-d2 / (2.0 * sigma * sigma)) * not_eye
        K_l = _row_stochastic_causal(A_l, causal_mask)
        K_g = _row_stochastic_causal(A_g, causal_mask)
        w_l = jax.nn.sigmoid(gate_logit)
        K = w_l * K_l + (1.0 - w_l) * K_g
        out = jnp.einsum('bnm,bmd->bnd', K, v)
        return jnp.einsum('bnd,ed->bne', out, W_O)

    def _L3_gnn_ref(h, causal_mask, W_lang, W_grav, W_V, W_O, gate_logit, log_sigma):
        import jax, jax.numpy as jnp
        import numpy as np
        EPS = 1e-08

        def _row_stochastic_causal(A, causal_mask):
            A = A * causal_mask
            deg = jnp.maximum(A.sum(axis=-1, keepdims=True), EPS)
            return A / deg
        z_l = jnp.einsum('bnd,ed->bne', h, W_lang)
        z_g = jnp.einsum('bnd,ed->bne', h, W_grav)
        v = jnp.einsum('bnd,ed->bne', h, W_V)
        N = h.shape[-2]
        not_eye = 1.0 - jnp.eye(N, dtype=h.dtype)
        zn = z_l / jnp.maximum(jnp.linalg.norm(z_l, axis=-1, keepdims=True), EPS)
        A_l = jnp.maximum(jnp.einsum('bnd,bmd->bnm', zn, zn), 0.0) * not_eye
        sq = jnp.sum(z_g * z_g, axis=-1, keepdims=True)
        d2 = jnp.maximum(sq + jnp.swapaxes(sq, -1, -2) - 2.0 * jnp.einsum('bnd,bmd->bnm', z_g, z_g), 0.0)
        sigma = jnp.exp(log_sigma)
        A_g = jnp.exp(-d2 / (2.0 * sigma * sigma)) * not_eye
        K_l = _row_stochastic_causal(A_l, causal_mask)
        K_g = _row_stochastic_causal(A_g, causal_mask)
        w_l = jax.nn.sigmoid(gate_logit)
        K = w_l * K_l + (1.0 - w_l) * K_g
        out = jnp.einsum('bnm,bmd->bnd', K, v)
        return jnp.einsum('bnd,ed->bne', out, W_O)
    x = _layernorm(x + _L0_gnn_ref(x, L0_gnn_wq, L0_gnn_wk, adj, L0_gnn_bm), axis=-1)
    x = _layernorm(x + _L1_gnn_ref(x, adj, adj, L1_gnn_bias), axis=-1)
    x = _layernorm(x + _L2_gnn_ref(x, adj, L2_gnn_W_lang, L2_gnn_W_grav, L2_gnn_W_V, L2_gnn_W_O, L2_gnn_gate_logit, L2_gnn_log_sigma), axis=-1)
    x = _layernorm(x + _L3_gnn_ref(x, adj, L3_gnn_W_lang, L3_gnn_W_grav, L3_gnn_W_V, L3_gnn_W_O, L3_gnn_gate_logit, L3_gnn_log_sigma), axis=-1)
    return x

_drawn_inputs = setup_inputs


def setup_inputs(seed=0):
    import zlib

    import numpy as np

    out = dict(_drawn_inputs(seed))
    spreads = {'L1_gnn_bias': (0.0, 0.1)}
    factors = {'L0_gnn_wq': 102.919, 'L0_gnn_wk': 134.935, 'L0_gnn_bm': 200.0}
    for name, (base, spread) in spreads.items():
        noise = np.random.default_rng([zlib.crc32(name.encode()), seed]).standard_normal(out[name].shape)
        drawn = base * np.exp(spread * noise) if base else spread * noise
        out[name] = jnp.asarray(drawn.astype(out[name].dtype))
    for name, factor in factors.items():
        out[name] = (out[name] * factor).astype(out[name].dtype)
    return out
```

```python
from contextlib import ExitStack

import concourse.bass as bass
from concourse import mybir

F32 = mybir.dt.float32
F32R = mybir.dt.float32r
ALU = mybir.AluOpType
ACT = mybir.ActivationFunctionType
AX = mybir.AxisListType

P = 128
LN_EPS = 1e-5
DEG_EPS = 1e-8
SLOPE = 0.01

HI, LO = 0, 1
PASSES = ((HI, HI), (LO, HI), (HI, LO))


def attention_and_hop(nc, setup, x, adj, adjT, columns, bias, out):
    BATCH, C, N = x.shape
    NC, NN = C // P, N // P
    YW = C + 2
    ident, ones, ones_r = setup["ident"], setup["ones"], setup["ones_r"]

    with ExitStack() as ctx:
        def sb(name, shape, dt=F32):
            return ctx.enter_context(nc.sbuf_tensor("a_" + name, shape, dt))

        def ps(name, shape):
            return ctx.enter_context(nc.psum_tensor("a_" + name, shape, F32))

        def sem(name):
            return ctx.enter_context(nc.semaphore("a_" + name))

        adjq = sb("adjq", [P, NC, YW])
        adjq2 = sb("adjq2", [P, 2, NC, YW], F32R)
        adjn = sb("adjn", [P, NC, C])
        hop = sb("hop", [P, NC, C])
        hop2 = sb("hop2", [P, 2, NC, C], F32R)
        cols = sb("cols", [P, 3, NC])
        wkb = sb("wkb", [P, NC, P])
        wkb2 = sb("wkb2", [P, 2, NC, P], F32R)
        biasb = sb("biasb", [P, N])
        nhalf = sb("nhalf", [P, 4])
        spare = sb("spare", [P, 1])

        x_in = sb("x_in", [P, NC, N])
        x2 = sb("x2", [P, 2, NC, N], F32R)
        x_res = sb("x_res", [P, NC, N])
        y2 = sb("y2", [P, 2, NN, C], F32R)
        qcol = sb("qcol", [P, NN])
        qtop = sb("qtop", [P, 1])
        qdiag = sb("qdiag", [P, P])
        qmax = sb("qmax", [P, 1])
        qs = sb("qs", [P, NN])
        ea = sb("ea", [P, NN])
        eb = sb("eb", [P, NN])
        karg = sb("karg", [P, 2, N])
        kexp = sb("kexp", [P, 2, N])
        e1 = sb("e1", [P, 2, N])
        e = sb("e", [P, 2, N])
        e2 = sb("e2", [P, 2, NN, N], F32R)
        rden = sb("rden", [P, N])
        o = sb("o", [P, NC, N])
        orelu = sb("orelu", [P, NC, N])
        s0 = sb("s0", [P, NC, N])
        stats = sb("stats", [P, 2, NC, 6])
        mv = sb("mv", [P, 2, NC, 2])
        ve = sb("ve", [P, 2, NC])
        rstd = sb("rstd", [P, 2, NC])
        nmean = sb("nmean", [P, 2, NC])
        nmr = sb("nmr", [P, 2, NC])
        x1 = sb("x1", [P, NC, N])
        x12 = sb("x12", [P, 2, NC, N], F32R)
        xb = sb("xb", [P, NC, N])
        s1 = sb("s1", [P, NC, N])
        yout = sb("yout", [P, NC, N])

        agg = ps("agg", [P, 3, N])
        kbank = ps("kbank", [P, N])
        ring = ps("ring", [P, 2, N])
        qbank = ps("qbank", [P, P])

        const_loaded = sem("const_loaded")
        const_step = sem("const_step")
        adjq_ready = sem("adjq_ready")
        wk_ready = sem("wk_ready")
        hop_ready = sem("hop_ready")
        nhalf_ready = sem("nhalf_ready")
        x_loaded = sem("x_loaded")
        xres_loaded = sem("xres_loaded")
        x_hi = sem("x_hi")
        x_lo = sem("x_lo")
        y_full = sem("y_full")
        y_hi = sem("y_hi")
        y_lo = sem("y_lo")
        q_copied = sem("q_copied")
        q_step = sem("q_step")
        k_full = sem("k_full")
        q_full = sem("q_full")
        karg_ready = sem("karg_ready")
        kexp_ready = sem("kexp_ready")
        qexp_ready = sem("qexp_ready")
        e1_ready = sem("e1_ready")
        e_ready = sem("e_ready")
        e_hi = sem("e_hi")
        e_lo_even = sem("e_lo_even")
        e_lo_odd = sem("e_lo_odd")
        agg_step = sem("agg_step")
        rden_ready = sem("rden_ready")
        o_ready = sem("o_ready")
        relu_ready = sem("relu_ready")
        s0_ready = sem("s0_ready")
        stats_ready = sem("stats_ready")
        mv_ready = sem("mv_ready")
        ve_ready = sem("ve_ready")
        ln_step = sem("ln_step")
        x1_ready = sem("x1_ready")
        x1_hi = sem("x1_hi")
        x1_lo = sem("x1_lo")
        xb_ready = sem("xb_ready")
        hop_full = sem("hop_full")
        s1_ready = sem("s1_ready")
        y_ready = sem("y_ready")
        y_stored = sem("y_stored")

        def nodes(ap):
            return ap.rearrange("(c p) f -> p c f", p=P)

        block = ctx.enter_context(nc.Block())

        @block.sync
        def _(sp):
            def load_x(j):
                sp.dma_start(x_in[:], nodes(x[j])).then_inc(x_loaded, 16)

            load_x(0)
            sp.dma_start(adjq[:, :, 0:C], nodes(adjT)).then_inc(const_loaded, 16)
            sp.dma_start(cols[:], columns).then_inc(const_loaded, 16)
            sp.dma_start(adjn[:], nodes(adj)).then_inc(const_loaded, 16)
            sp.dma_start(biasb[:], bias.partition_broadcast(P)).then_inc(const_loaded, 16)

            def step(j, coming):
                sp.wait_ge(s0_ready, NC * j)
                sp.dma_start(x_res[:], nodes(x[j])).then_inc(xres_loaded, 16)
                sp.wait_ge(x_lo, j + 1)
                load_x(coming)
                sp.wait_ge(y_ready, NC * j + NC)
                sp.dma_start(nodes(out[j]), yout[:]).then_inc(y_stored, 16)

            with sp.Fori(0, BATCH - 1) as j:
                step(j, j + 1)
            step(BATCH - 1, 0)
            sp.wait_ge(y_stored, 16 * BATCH)
            sp.wait_ge(x_loaded, 16 * BATCH + 16)

        @block.gpsimd
        def _(pool):
            nc.gpsimd.memset(nhalf[:], -0.5).then_inc(nhalf_ready, 1)
            pool.wait_ge(nhalf_ready, 1)

            def split_x(n):
                pool.wait_ge(x_hi, n + 1)
                nc.gpsimd.tensor_tensor(x2[:, LO], x_in[:], x2[:, HI].bitcast(F32), ALU.subtract).then_inc(x_lo, 1)

            def e_low(n, c):
                pool.wait_ge(e_hi, NN * n + c + 1)
                nc.gpsimd.tensor_tensor(e2[:, LO, c], e[:, c % 2], e2[:, HI, c].bitcast(F32),
                                        ALU.subtract).then_inc(e_lo_odd, 1)

            def norm_scalars(which, j):
                pool.wait_ge(ve_ready, 4 * j + 2 * which + 2)
                nc.gpsimd.tensor_tensor(rstd[:, which], ve[:, which], nhalf[:, 0:NC], ALU.pow).then_inc(ln_step, 1)
                pool.wait_ge(ln_step, 4 * j + 2 * which + 1)
                nc.gpsimd.tensor_tensor(nmr[:, which], nmean[:, which], rstd[:, which], ALU.mult).then_inc(ln_step, 1)

            split_x(0)
            for c in (1, 3):
                e_low(0, c)
            with pool.Fori(0, BATCH) as j:
                split_x(j + 1)
                for c in range(NC):
                    pool.wait_ge(relu_ready, NC * j + c + 1)
                    if c == 0:
                        pool.wait_ge(xres_loaded, 16 * j + 16)
                    nc.gpsimd.tensor_tensor(s0[:, c], orelu[:, c], x_res[:, c], ALU.add).then_inc(s0_ready, 1)
                norm_scalars(0, j)
                for c in range(NC):
                    pool.wait_ge(x1_ready, NC * j + c + 1)
                    nc.gpsimd.tensor_tensor(xb[:, c], x1[:, c], biasb[:], ALU.add).then_inc(xb_ready, 1)
                for c in (1, 3):
                    e_low(j + 1, c)
                norm_scalars(1, j)

        @block.scalar
        def _(act):
            def y_high(n):
                for c in range(NN):
                    act.wait_ge(y_full, NN * n + c + 1)
                    nc.scalar.activation(y2[:, HI, c], ring[:, c % 2, 0:C], ACT.Copy).then_inc(y_hi, 1)

            def exponentials(n):
                act.wait_ge(q_step, 5 * n + 4)
                nc.scalar.activation(ea[:], qs[:], ACT.Exp).then_inc(qexp_ready, 1)
                nc.scalar.activation(eb[:], qs[:], ACT.Exp, scale=SLOPE).then_inc(qexp_ready, 1)
                for i, scale in ((0, 1.0 - SLOPE), (1, SLOPE - 1.0)):
                    act.wait_ge(karg_ready, 2 * n + i + 1)
                    nc.scalar.activation(kexp[:, i], karg[:, i], ACT.Exp, scale=scale).then_inc(kexp_ready, 1)

            def e_first(n, c):
                if c == 0:
                    act.wait_ge(kexp_ready, 2 * n + 1)
                    act.wait_ge(qexp_ready, 2 * n + 2)
                nc.scalar.activation(e1[:, c % 2], kexp[:, 0], ACT.Copy, scale=ea[:, c:c + 1]).then_inc(e1_ready, 1)

            def e_high(n, c):
                act.wait_ge(e_ready, NN * n + c + 1)
                if c == 0:
                    act.wait_ge(agg_step, NN * n)
                nc.scalar.activation(e2[:, HI, c], e[:, c % 2], ACT.Copy).then_inc(e_hi, 1)

            def e_chunks(n):
                e_first(n, 0)
                e_first(n, 1)
                e_high(n, 0)
                e_first(n, 2)
                e_high(n, 1)
                e_first(n, 3)
                e_high(n, 2)
                e_high(n, 3)

            y_high(0)
            exponentials(0)
            e_chunks(0)
            with act.Fori(0, BATCH) as j:
                for c in range(NC):
                    act.wait_ge(o_ready, NC * j + c + 1)
                    nc.scalar.activation(orelu[:, c], o[:, c], ACT.Relu, bias=cols[:, 2, c:c + 1]).then_inc(relu_ready, 1)
                y_high(j + 1)
                act.wait_ge(ln_step, 4 * j + 2)
                for c in range(NC):
                    nc.scalar.activation(x1[:, c], s0[:, c], ACT.Identity, bias=nmr[:, 0, c:c + 1],
                                         scale=rstd[:, 0, c:c + 1]).then_inc(x1_ready, 1)
                exponentials(j + 1)
                e_chunks(j + 1)
                act.wait_ge(ln_step, 4 * j + 4)
                act.wait_ge(y_stored, 16 * j)
                for c in range(NC):
                    nc.scalar.activation(yout[:, c], s1[:, c], ACT.Identity, bias=nmr[:, 1, c:c + 1],
                                         scale=rstd[:, 1, c:c + 1]).then_inc(y_ready, 1)

        @block.vector
        def _(dve):
            steps = [0]

            def step(ins):
                steps[0] += 1
                ins.then_inc(const_step, 1)
                dve.wait_ge(const_step, steps[0])

            step(nc.vector.memset(adjq[:, :, C + 1:C + 2], 0.0))
            dve.wait_ge(const_loaded, 16 * 4)
            step(nc.vector.tensor_copy(adjq[:, :, C], cols[:, 0]))
            step(nc.vector.tensor_copy(adjq2[:, HI], adjq[:]))
            nc.vector.tensor_tensor(adjq2[:, LO], adjq[:], adjq2[:, HI].bitcast(F32),
                                    ALU.subtract).then_inc(adjq_ready, 1)

            def x_high(n):
                dve.wait_ge(x_loaded, 16 * n + 16)
                dve.wait_ge(k_full, n)
                nc.vector.tensor_copy(x2[:, HI], x_in[:]).then_inc(x_hi, 1)

            x_high(0)
            for c in range(NC):
                step(nc.vector.tensor_scalar(wkb[:, c], ones[:], cols[:, 1, c:c + 1], None, ALU.mult))
            step(nc.vector.tensor_copy(wkb2[:, HI], wkb[:]))
            nc.vector.tensor_tensor(wkb2[:, LO], wkb[:], wkb2[:, HI].bitcast(F32), ALU.subtract).then_inc(wk_ready, 1)
            step(nc.vector.tensor_tensor(hop[:], adjn[:], adjn[:], ALU.mult))
            step(nc.vector.tensor_copy(hop2[:, HI], hop[:]))
            nc.vector.tensor_tensor(hop2[:, LO], hop[:], hop2[:, HI].bitcast(F32), ALU.subtract).then_inc(hop_ready, 1)

            def y_low(n):
                for c in range(NN):
                    dve.wait_ge(y_hi, NN * n + c + 1)
                    nc.vector.tensor_copy(qcol[:, c:c + 1], ring[:, c % 2, C:C + 1]).then_inc(q_copied, 1)
                    nc.vector.tensor_tensor(y2[:, LO, c], ring[:, c % 2, 0:C], y2[:, HI, c].bitcast(F32),
                                            ALU.subtract).then_inc(y_lo, 1)

            def q_diagonal(n):
                dve.wait_ge(q_copied, NN * n + NN)
                nc.vector.tensor_reduce(qtop[:], qcol[:], AX.X, ALU.max).then_inc(q_step, 1)
                dve.wait_ge(q_step, 5 * n + 1)
                nc.vector.tensor_scalar(qdiag[:], ident[:], qtop[:], None, ALU.mult).then_inc(q_step, 1)

            def q_and_k(n):
                dve.wait_ge(q_full, n + 1)
                nc.vector.tensor_reduce(qmax[:], qbank[:], AX.X, ALU.max).then_inc(q_step, 1)
                dve.wait_ge(q_step, 5 * n + 3)
                nc.vector.tensor_scalar(qs[:], qcol[:], qmax[:], None, ALU.subtract).then_inc(q_step, 1)
                dve.wait_ge(k_full, n + 1)
                dve.wait_ge(kexp_ready, 2 * n)
                nc.vector.tensor_scalar(karg[:, 0], kbank[:], qmax[:], 0.0, ALU.add, ALU.min).then_inc(karg_ready, 1)
                nc.vector.tensor_scalar(karg[:, 1], kbank[:], qmax[:], 0.0, ALU.add, ALU.max).then_inc(karg_ready, 1)
                nc.vector.tensor_copy(qdiag[:, 0:1], qmax[:]).then_inc(q_step, 1)

            def e_max(n, c):
                dve.wait_ge(e1_ready, NN * n + c + 1)
                if c == 0:
                    dve.wait_ge(kexp_ready, 2 * n + 2)
                if c % 2 == 0:
                    dve.wait_ge(e_lo_even, 2 * n + c // 2)
                else:
                    dve.wait_ge(e_lo_odd, 2 * n + c // 2)
                nc.vector.scalar_tensor_tensor(out=e[:, c % 2], in0=kexp[:, 1], scalar=eb[:, c:c + 1],
                                               in1=e1[:, c % 2], op0=ALU.mult, op1=ALU.max).then_inc(e_ready, 1)

            def e_low(n, c):
                dve.wait_ge(e_hi, NN * n + c + 1)
                nc.vector.tensor_tensor(e2[:, LO, c], e[:, c % 2], e2[:, HI, c].bitcast(F32),
                                        ALU.subtract).then_inc(e_lo_even, 1)

            def e_chunks(n):
                e_max(n, 0)
                e_max(n, 1)
                e_low(n, 0)
                e_max(n, 2)
                e_max(n, 3)
                e_low(n, 2)

            def row_stats(which, j, ready):
                for c in range(NC):
                    dve.wait_ge(ready, NC * j + c + 1)
                    nc.vector.bn_stats(stats[:, which, c], (s0, s1)[which][:, c]).then_inc(stats_ready, 1)
                dve.wait_ge(stats_ready, 2 * NC * j + NC * which + NC)
                nc.vector.memset(spare[:], 0.0)
                for c in range(NC):
                    nc.vector.bn_aggr(mv[:, which, c], stats[:, which, c]).then_inc(mv_ready, 1)
                dve.wait_ge(mv_ready, 2 * NC * j + NC * which + NC)
                nc.vector.tensor_scalar(ve[:, which], mv[:, which, :, 1], LN_EPS, None, ALU.add).then_inc(ve_ready, 1)
                nc.vector.tensor_scalar(nmean[:, which], mv[:, which, :, 0], -1.0, None, ALU.mult).then_inc(ve_ready, 1)

            y_low(0)
            q_diagonal(0)
            q_and_k(0)
            e_chunks(0)
            with dve.Fori(0, BATCH) as j:
                x_high(j + 1)
                dve.wait_ge(agg_step, NN * j + NN)
                nc.vector.reciprocal(rden[:], agg[:, 2]).then_inc(rden_ready, 1)
                dve.wait_ge(rden_ready, j + 1)
                for c in range(NC):
                    nc.vector.tensor_tensor(o[:, c], agg[:, c], rden[:], ALU.mult).then_inc(o_ready, 1)
                y_low(j + 1)
                q_diagonal(j + 1)
                row_stats(0, j, s0_ready)
                for c in range(NC):
                    dve.wait_ge(x1_ready, NC * j + c + 1)
                    nc.vector.tensor_copy(x12[:, HI, c], x1[:, c]).then_inc(x1_hi, 1)
                for c in range(NC):
                    dve.wait_ge(x1_hi, NC * j + c + 1)
                    nc.vector.tensor_tensor(x12[:, LO, c], x1[:, c], x12[:, HI, c].bitcast(F32),
                                            ALU.subtract).then_inc(x1_lo, 1)
                q_and_k(j + 1)
                e_chunks(j + 1)
                for c in range(NC):
                    dve.wait_ge(hop_full, NC * j + c + 1)
                    dve.wait_ge(xb_ready, NC * j + c + 1)
                    if c == 0:
                        dve.wait_ge(y_ready, NC * j)
                    nc.vector.tensor_tensor(s1[:, c], ring[:, c % 2], xb[:, c], ALU.add).then_inc(s1_ready, 1)
                row_stats(1, j, s1_ready)

        @block.tensor
        def _(pe):
            def transposed_products(n):
                pe.wait_ge(x_lo, n + 1)
                for c in range(NN):
                    if c >= 2:
                        pe.wait_ge(y_lo, NN * n + c - 1)
                    mm = 0
                    for l, r in PASSES:
                        for k in range(NC):
                            ins = nc.tensor.matmul(ring[:, c % 2, 0:YW], x2[:, l, k, c * P:(c + 1) * P],
                                                   adjq2[:, r, k], start=(mm == 0), stop=(mm == 3 * NC - 1))
                            mm += 1
                    ins.then_inc(y_full, 1)

            def keys(n):
                pe.wait_ge(karg_ready, 2 * n)
                mm = 0
                for l, r in PASSES:
                    for k in range(NC):
                        ins = nc.tensor.matmul(kbank[:], wkb2[:, l, k], x2[:, r, k],
                                               start=(mm == 0), stop=(mm == 3 * NC - 1))
                        mm += 1
                ins.then_inc(k_full, 1)

            def spread_q(n):
                pe.wait_ge(q_step, 5 * n + 2)
                nc.tensor.matmul(qbank[:], ones[:], qdiag[:], start=True, stop=True).then_inc(q_full, 1)

            pe.wait_ge(adjq_ready, 1)
            transposed_products(0)
            pe.wait_ge(wk_ready, 1)
            keys(0)
            spread_q(0)
            pe.wait_ge(hop_ready, 1)
            with pe.Fori(0, BATCH) as j:
                pe.wait_ge(o_ready, NC * j)
                pe.wait_ge(y_lo, NN * j + NN)
                for c in range(NN):
                    pe.wait_ge(e_hi, NN * j + c + 1)
                    if c % 2:
                        pe.wait_ge(e_lo_odd, 2 * j + c // 2 + 1)
                    else:
                        pe.wait_ge(e_lo_even, 2 * j + c // 2 + 1)
                    for i in range(NC):
                        for l, r in PASSES:
                            nc.tensor.matmul(agg[:, i], y2[:, l, c, i * P:(i + 1) * P], e2[:, r, c],
                                             start=(c == 0 and (l, r) == PASSES[0]),
                                             stop=(c == NN - 1 and (l, r) == PASSES[-1]))
                    for r in (HI, LO):
                        ins = nc.tensor.matmul(agg[:, 2], ones_r[:], e2[:, r, c],
                                               start=(c == 0 and r == HI), stop=(c == NN - 1 and r == LO))
                    ins.then_inc(agg_step, 1)
                pe.wait_ge(s1_ready, NC * j)
                transposed_products(j + 1)
                keys(j + 1)
                pe.wait_ge(y_lo, NN * j + 2 * NN)
                spread_q(j + 1)
                for m in range(NC):
                    mm = 0
                    for k in range(NC):
                        if m == 0:
                            pe.wait_ge(x1_lo, NC * j + k + 1)
                        for l, r in PASSES:
                            ins = nc.tensor.matmul(ring[:, m % 2], hop2[:, l, k, m * P:(m + 1) * P], x12[:, r, k],
                                                   start=(mm == 0), stop=(mm == 3 * NC - 1))
                            mm += 1
                    ins.then_inc(hop_full, 1)


def kernel_similarity_layers(nc, setup, adj, wlT, wgT, wv, woT, gate, log_sigma, out):
    LAYERS = wlT.shape[0]
    BATCH, C, D = out.shape
    B = 2
    NC, ND = C // P, D // P
    PAIRS = BATCH // B
    ROWS = B * C
    BC = B * NC
    ident, ones_r = setup["ident"], setup["ones_r"]

    with ExitStack() as ctx:
        def sb(name, shape, dt=F32):
            return ctx.enter_context(nc.sbuf_tensor("l_" + name, shape, dt))

        def ps(name, shape):
            return ctx.enter_context(nc.psum_tensor("l_" + name, shape, F32))

        def sem(name):
            return ctx.enter_context(nc.semaphore("l_" + name))

        stage_a = sb("stage_a", [P, ND, D])
        stage_b = sb("stage_b", [P, ND, D])
        wz2 = [sb("wl2", [P, 2, ND, D], F32R), sb("wg2", [P, 2, ND, D], F32R)]
        wvo2 = sb("wvo2", [P, 2, ND, D], F32R)
        adj_off = sb("adj_off", [P, NC, C])
        gate_in = sb("gate_in", [P, LAYERS])
        sigma_in = sb("sigma_in", [P, LAYERS])
        small = sb("small", [P, 8])
        spare = sb("spare", [P, 1])
        inv_s2 = sb("inv_s2", [P, 1])
        w_l = sb("w_l", [P, 1])
        expo = sb("expo", [P, BC])

        x_tr = sb("x_tr", [P, BC, D])
        x_res = sb("x_res", [P, BC, D])
        xT2 = sb("xT2", [P, 2, ND, ROWS], F32R)
        z2 = [sb("zl2", [P, 2, ND, ROWS], F32R), sb("zg2", [P, 2, ND, ROWS], F32R)]
        v2 = sb("v2", [P, 2, BC, D], F32R)
        sq = sb("sq", [P, 2, BC])
        sqm = sb("sqm", [P, BC])
        rn = sb("rn", [P, BC])
        gbias = sb("gbias", [P, BC])
        diag = sb("diag", [P, 2, BC, P])
        diag2 = sb("diag2", [P, 2, 2, BC, P], F32R)
        adj_r = sb("adj_r", [P, B, NC, C])
        e_g = sb("e_g", [P, BC, C])
        t_l = sb("t_l", [P, BC, C])
        t_g = sb("t_g", [P, BC, C])
        deg = sb("deg", [P, 2 * BC])
        dm = sb("dm", [P, 2 * BC])
        drec = sb("drec", [P, 2 * BC])
        coef = sb("coef", [P, 2 * BC])
        cnorm = sb("cnorm", [P, 2 * BC])
        km = sb("km", [P, BC, C])
        kT2 = sb("kT2", [P, 2, B, NC, C], F32R)
        s = sb("s", [P, BC, D])
        stats = sb("stats", [P, BC, 6])
        mv = sb("mv", [P, BC, 2])
        ve = sb("ve", [P, BC])
        rstd = sb("rstd", [P, BC])
        nmean = sb("nmean", [P, BC])
        nmr = sb("nmr", [P, BC])

        ring = ps("ring", [P, 2, 512])
        gram = ps("gram", [P, 2, B, NC, C])
        rbank = ps("rbank", [P, B, C])
        tbank = ps("tbank", [P, NC, C])

        consts_loaded = sem("consts_loaded")
        const_step = sem("const_step")
        expo_ready = sem("expo_ready")
        vo_loaded = sem("vo_loaded")
        z_loaded = sem("z_loaded")
        wvo_full = sem("wvo_full")
        w_hi = sem("w_hi")
        w_lo = sem("w_lo")
        scalar_exp = sem("scalar_exp")
        scalar_step = sem("scalar_step")
        coef_ready = sem("coef_ready")
        xtr_loaded = sem("xtr_loaded")
        xres_loaded = sem("xres_loaded")
        ring_full = sem("ring_full")
        hi_ready = sem("hi_ready")
        lo_ready = sem("lo_ready")
        gram_full = sem("gram_full")
        diag_ready = sem("diag_ready")
        sqm_ready = sem("sqm_ready")
        rn_ready = sem("rn_ready")
        gbias_ready = sem("gbias_ready")
        dl_ready = sem("dl_ready")
        dhi_ready = sem("dhi_ready")
        dlo_ready = sem("dlo_ready")
        r_full = sem("r_full")
        sq_added = sem("sq_added")
        adjr_ready = sem("adjr_ready")
        tl_ready = sem("tl_ready")
        eg_ready = sem("eg_ready")
        tg_ready = sem("tg_ready")
        coef_step = sem("coef_step")
        ve_ready = sem("ve_ready")
        scaled = sem("scaled")
        k_ready = sem("k_ready")
        kt_full = sem("kt_full")
        kt_hi = sem("kt_hi")
        kt_lo = sem("kt_lo")
        s_ready = sem("s_ready")
        stats_ready = sem("stats_ready")
        mv_ready = sem("mv_ready")
        ln_step = sem("ln_step")
        y_ready = sem("y_ready")
        y_stored = sem("y_stored")

        def weight(w):
            return w.rearrange("(k p) e -> p k e", p=P)

        def pair_rows(pair):
            return out.rearrange("(g b) (c p) f -> g p (b c) f", b=B, p=P)[pair]

        SPLITS = 4 * ND
        Z0, V0, T0 = 0, 2 * ND, 2 * ND + BC

        def splits(u, n):
            return ND + SPLITS * u + n

        RING = SPLITS + BC
        TAIL = ("t0", "t1", "k0", "k1", "k2", "t2", "k3", "t3")

        def filled(u, n):
            return ND + RING * u + n

        def tail_at(name):
            return V0 + BC + TAIL.index(name)

        block = ctx.enter_context(nc.Block())

        @block.sync
        def _(sp):
            sp.dma_start(adj_off[:], adj.rearrange("(c p) f -> p c f", p=P)).then_inc(consts_loaded, 16)
            sp.dma_start(gate_in[:], gate.partition_broadcast(P)).then_inc(consts_loaded, 16)
            sp.dma_start(sigma_in[:], log_sigma.partition_broadcast(P)).then_inc(consts_loaded, 16)
            sp.dma_start(x_tr[:], pair_rows(0)).then_inc(xtr_loaded, 16)
            for layer in range(LAYERS):
                if layer:
                    sp.wait_ge(w_lo, 3 * layer)
                sp.dma_start(stage_a[:], weight(wv[layer])).then_inc(vo_loaded, 16)
                sp.dma_start(stage_b[:], weight(woT[layer])).then_inc(vo_loaded, 16)
                if layer == 0:
                    sp.wait_ge(wvo_full, 1)
                    sp.dma_start(stage_a[:], weight(wlT[layer])).then_inc(z_loaded, 16)
                    sp.dma_start(stage_b[:], weight(wgT[layer])).then_inc(z_loaded, 16)
                    sp.wait_ge(w_lo, 3)
                else:
                    sp.wait_ge(wvo_full, layer + 1)
                    sp.dma_start(stage_a[:], weight(wlT[layer])).then_inc(z_loaded, 16)
                    sp.dma_start(stage_b[:], weight(wgT[layer])).then_inc(z_loaded, 16)

                def step(u, pair, coming):
                    sp.wait_ge(y_stored, 16 * B * u)
                    sp.dma_start(x_res[:], pair_rows(pair)).then_inc(xres_loaded, 16)
                    sp.wait_ge(lo_ready, splits(u, 0))
                    sp.dma_start(x_tr[:], pair_rows(coming)).then_inc(xtr_loaded, 16)
                    for b in range(B):
                        sp.wait_ge(y_ready, BC * u + NC * (b + 1))
                        sp.dma_start(pair_rows(pair)[:, NC * b:NC * (b + 1)],
                                     s[:, NC * b:NC * (b + 1)]).then_inc(y_stored, 16)

                with sp.Fori(0, PAIRS - 1) as pair:
                    step(layer * PAIRS + pair, pair, pair + 1)
                step(layer * PAIRS + PAIRS - 1, PAIRS - 1, 0)
            sp.wait_ge(y_stored, 16 * B * LAYERS * PAIRS)
            sp.wait_ge(xtr_loaded, 16 * (LAYERS * PAIRS + 1))

        @block.gpsimd
        def _(pool):
            nc.gpsimd.memset(expo[:], -0.5).then_inc(expo_ready, 1)
            pool.wait_ge(expo_ready, 1)
            with pool.Fori(0, LAYERS) as layer:
                with pool.Fori(0, PAIRS) as pair:
                    u = layer * PAIRS + pair

                    pool.wait_ge(sqm_ready, u + 1)
                    nc.gpsimd.tensor_tensor(rn[:], sqm[:], expo[:, 0:BC], ALU.pow).then_inc(rn_ready, 1)
                    for b in range(B):
                        of = slice(NC * b, NC * (b + 1))
                        pool.wait_ge(ve_ready, 2 * (B * u + b) + 2)
                        nc.gpsimd.tensor_tensor(rstd[:, of], ve[:, of], expo[:, of], ALU.pow).then_inc(ln_step, 1)
                        pool.wait_ge(ln_step, 2 * (B * u + b) + 1)
                        nc.gpsimd.tensor_tensor(nmr[:, of], nmean[:, of], rstd[:, of], ALU.mult).then_inc(ln_step, 1)

        @block.scalar
        def _(act):
            def high(out_, in_, nth_full, bank):
                act.wait_ge(ring_full, nth_full)
                nc.scalar.activation(out_, ring[:, bank], ACT.Copy).then_inc(hi_ready, 1)

            for t in range(ND):
                high(xT2[:, HI, t], None, t + 1, t % 2)
            with act.Fori(0, LAYERS) as layer:
                act.wait_ge(scalar_step, 6 * layer + 2)
                nc.scalar.activation(small[:, 2:3], small[:, 0:1], ACT.Exp, scale=-1.0).then_inc(scalar_exp, 1)
                nc.scalar.activation(inv_s2[:], small[:, 1:2], ACT.Exp, scale=-2.0).then_inc(scalar_exp, 1)
                act.wait_ge(wvo_full, layer + 1)
                nc.scalar.activation(wvo2[:, HI], gram[:].rearrange("p g b c f -> p (g b) (c f)"),
                                     ACT.Copy).then_inc(w_hi, 1)
                for i, stage in enumerate((stage_a, stage_b)):
                    act.wait_ge(z_loaded, 32 * layer + 32)
                    nc.scalar.activation(wz2[i][:, HI], stage[:], ACT.Copy).then_inc(w_hi, 1)
                with act.Fori(0, PAIRS) as pair:
                    u = layer * PAIRS + pair

                    def exps(b):
                        act.wait_ge(sq_added, B * u + b + 1)
                        act.wait_ge(gbias_ready, B * u + b + 1)
                        for c in range(NC):
                            i = NC * b + c
                            nc.scalar.activation(e_g[:, i], gram[:, 1, b, c], ACT.Exp, bias=gbias[:, i:i + 1],
                                                 scale=inv_s2[:]).then_inc(eg_ready, 1)

                    for i in range(2 * ND):
                        high(z2[i // ND][:, HI, i % ND], None, filled(u, i + 1), i % 2)
                    for i in range(BC):
                        high(v2[:, HI, i], None, filled(u, V0 + i + 1), i % 2)
                        if i >= 1 and i < 3:
                            exps(i - 1)
                    for t in (0, 1):
                        high(xT2[:, HI, t], None, filled(u, tail_at(f"t{t}") + 1), tail_at(f"t{t}") % 2)
                    for b in range(B):
                        act.wait_ge(kt_full, B * u + b + 1)
                        nc.scalar.activation(kT2[:, HI, b], tbank[:], ACT.Copy).then_inc(kt_hi, 1)
                    for t in (2, 3):
                        high(xT2[:, HI, t], None, filled(u, tail_at(f"t{t}") + 1), tail_at(f"t{t}") % 2)
                    for b in range(B):
                        act.wait_ge(ln_step, 2 * (B * u + b) + 2)
                        for i in range(NC * b, NC * (b + 1)):
                            nc.scalar.activation(s[:, i], s[:, i], ACT.Identity, bias=nmr[:, i:i + 1],
                                                 scale=rstd[:, i:i + 1]).then_inc(y_ready, 1)

        @block.vector
        def _(dve):
            steps = [0]

            def step(ins):
                steps[0] += 1
                ins.then_inc(const_step, 1)
                dve.wait_ge(const_step, steps[0])

            dve.wait_ge(consts_loaded, 48)
            for c in range(NC):
                block_ = adj_off[:, c, c * P:(c + 1) * P]
                step(nc.vector.tensor_tensor(diag[:, 0, c], block_, ident[:], ALU.mult))
                step(nc.vector.tensor_tensor(block_, block_, diag[:, 0, c], ALU.subtract))

            def low(out_, hi, nth_hi, bank):
                dve.wait_ge(hi_ready, nth_hi)
                nc.vector.tensor_tensor(out_, ring[:, bank], hi.bitcast(F32), ALU.subtract).then_inc(lo_ready, 1)

            for t in range(ND):
                low(xT2[:, LO, t], xT2[:, HI, t], t + 1, t % 2)
            with dve.Fori(0, LAYERS) as layer:
                def scalar(ins, n):
                    ins.then_inc(scalar_step, 1)
                    dve.wait_ge(scalar_step, 6 * layer + n)

                scalar(nc.vector.tensor_copy(small[:, 0:1], gate_in[:, bass.ds(layer, 1)]), 1)
                scalar(nc.vector.tensor_copy(small[:, 1:2], sigma_in[:, bass.ds(layer, 1)]), 2)
                dve.wait_ge(scalar_exp, 2 * layer + 1)
                scalar(nc.vector.tensor_scalar(small[:, 3:4], small[:, 2:3], 1.0, None, ALU.add), 3)
                scalar(nc.vector.reciprocal(w_l[:], small[:, 3:4]), 4)
                scalar(nc.vector.tensor_scalar(small[:, 4:5], w_l[:], -1.0, 1.0, ALU.mult, ALU.add), 5)
                dve.wait_ge(expo_ready, 1)
                scalar(nc.vector.tensor_scalar(coef[:, BC:2 * BC], expo[:, 0:BC], 0.0, small[:, 4:5],
                                               ALU.mult, ALU.add), 6)
                dve.wait_ge(scalar_exp, 2 * layer + 2)
                nc.vector.tensor_copy(small[:, 5:6], inv_s2[:]).then_inc(coef_ready, 1)
                dve.wait_ge(w_hi, 3 * layer + 1)
                nc.vector.tensor_tensor(wvo2[:, LO], gram[:].rearrange("p g b c f -> p (g b) (c f)"),
                                        wvo2[:, HI].bitcast(F32), ALU.subtract).then_inc(w_lo, 1)
                for i, stage in enumerate((stage_a, stage_b)):
                    dve.wait_ge(w_hi, 3 * layer + 2 + i)
                    nc.vector.tensor_tensor(wz2[i][:, LO], stage[:], wz2[i][:, HI].bitcast(F32),
                                            ALU.subtract).then_inc(w_lo, 1)
                with dve.Fori(0, PAIRS) as pair:
                    u = layer * PAIRS + pair

                    def diagonals(g, b):
                        dve.wait_ge(gram_full, 2 * B * u + B * g + b + 1)
                        for c in range(NC):
                            i = NC * b + c
                            nc.vector.tensor_tensor_reduce(
                                out=diag[:, g, i], in0=gram[:, g, b, c, c * P:(c + 1) * P], in1=ident[:],
                                scale=(1.0, -0.5)[g], scalar=0.0, op0=ALU.mult, op1=ALU.add,
                                accum_out=sq[:, g, i:i + 1]).then_inc(diag_ready, 1)

                    def gaussian_bias(b):
                        of = slice(NC * b, NC * (b + 1))
                        dve.wait_ge(diag_ready, 2 * BC * u + BC + NC * (b + 1))
                        nc.vector.tensor_scalar(gbias[:, of], sq[:, 1, of], inv_s2[:], None,
                                                ALU.mult).then_inc(gbias_ready, 1)

                    def coefs(ins, n):
                        ins.then_inc(coef_step, 1)
                        dve.wait_ge(coef_step, 5 * u + n)

                    def split_diag(g, of, nth, ready, count):
                        dve.wait_ge(ready, count)
                        nc.vector.tensor_copy(diag2[:, g, HI, of], diag[:, g, of]).then_inc(dhi_ready, 1)
                        dve.wait_ge(dhi_ready, (B + 1) * u + nth)
                        nc.vector.tensor_tensor(diag2[:, g, LO, of], diag[:, g, of],
                                                diag2[:, g, HI, of].bitcast(F32), ALU.subtract).then_inc(dlo_ready, 1)

                    def v_low(i):
                        low(v2[:, LO, i], v2[:, HI, i], splits(u, V0 + i + 1), i % 2)

                    def cosines(b):
                        dve.wait_ge(r_full, u + 1)
                        for c in range(NC):
                            nc.vector.tensor_tensor(adj_r[:, b, c], rbank[:, b], adj_off[:, c],
                                                    ALU.mult).then_inc(adjr_ready, 1)
                        for c in range(NC):
                            i = NC * b + c
                            dve.wait_ge(adjr_ready, BC * u + i + 1)
                            nc.vector.scalar_tensor_tensor(
                                out=t_l[:, i], in0=gram[:, 0, b, c], scalar=0.0, in1=adj_r[:, b, c],
                                op0=ALU.max, op1=ALU.mult, accum_out=deg[:, i:i + 1]).then_inc(tl_ready, 1)

                    def gaussians(b):
                        for c in range(NC):
                            i = NC * b + c
                            dve.wait_ge(eg_ready, BC * u + i + 1)
                            nc.vector.scalar_tensor_tensor(
                                out=t_g[:, i], in0=e_g[:, i], scalar=1.0, in1=adj_off[:, c],
                                op0=ALU.min, op1=ALU.mult, accum_out=deg[:, BC + i:BC + i + 1]).then_inc(tg_ready, 1)

                    def combine(b):
                        for i in range(NC * b, NC * (b + 1)):
                            nc.vector.tensor_scalar(t_g[:, i], t_g[:, i], cnorm[:, BC + i:BC + i + 1], None,
                                                    ALU.mult).then_inc(scaled, 1)
                        for i in range(NC * b, NC * (b + 1)):
                            dve.wait_ge(scaled, BC * u + i + 1)
                            nc.vector.scalar_tensor_tensor(out=km[:, i], in0=t_l[:, i], scalar=cnorm[:, i:i + 1],
                                                           in1=t_g[:, i], op0=ALU.mult, op1=ALU.add).then_inc(k_ready, 1)

                    def x_low(t):
                        low(xT2[:, LO, t], xT2[:, HI, t], splits(u, T0 + t + 1), tail_at(f"t{t}") % 2)

                    def kt_low(b):
                        dve.wait_ge(kt_hi, B * u + b + 1)
                        nc.vector.tensor_tensor(kT2[:, LO, b], tbank[:], kT2[:, HI, b].bitcast(F32),
                                                ALU.subtract).then_inc(kt_lo, 1)

                    def residual(i):
                        at = tail_at(f"k{i}")
                        dve.wait_ge(ring_full, filled(u, at + 1))
                        if i == 0:
                            dve.wait_ge(xres_loaded, 16 * u + 16)
                        if i % NC == 0:
                            dve.wait_ge(y_stored, 16 * B * u)
                        nc.vector.tensor_tensor(s[:, i], ring[:, at % 2], x_res[:, i], ALU.add).then_inc(s_ready, 1)

                    def row_stats(i):
                        dve.wait_ge(s_ready, BC * u + i + 1)
                        nc.vector.bn_stats(stats[:, i], s[:, i]).then_inc(stats_ready, 1)

                    def row_moments(b):
                        of = slice(NC * b, NC * (b + 1))
                        dve.wait_ge(stats_ready, BC * u + NC * (b + 1))
                        nc.vector.memset(spare[:], 0.0)
                        for i in range(NC * b, NC * (b + 1)):
                            nc.vector.bn_aggr(mv[:, i], stats[:, i]).then_inc(mv_ready, 1)
                        dve.wait_ge(mv_ready, BC * u + NC * (b + 1))
                        nc.vector.tensor_scalar(ve[:, of], mv[:, of, 1], LN_EPS, None, ALU.add).then_inc(ve_ready, 1)
                        nc.vector.tensor_scalar(nmean[:, of], mv[:, of, 0], -1.0, None, ALU.mult).then_inc(ve_ready, 1)

                    for i in range(2 * ND):
                        z = z2[i // ND]
                        low(z[:, LO, i % ND], z[:, HI, i % ND], splits(u, i + 1), i % 2)
                    diagonals(0, 0)
                    diagonals(0, 1)
                    dve.wait_ge(diag_ready, 2 * BC * u + BC)
                    nc.vector.tensor_scalar(sqm[:], sq[:, 0], DEG_EPS * DEG_EPS, None, ALU.max).then_inc(sqm_ready, 1)
                    diagonals(1, 0)
                    gaussian_bias(0)
                    split_diag(1, slice(0, NC), 1, diag_ready, 2 * BC * u + BC + NC)
                    dve.wait_ge(rn_ready, u + 1)
                    for i in range(BC):
                        nc.vector.tensor_scalar(diag[:, 0, i], ident[:], rn[:, i:i + 1], None,
                                                ALU.mult).then_inc(dl_ready, 1)
                    split_diag(0, slice(0, BC), 2, dl_ready, BC * u + BC)
                    coefs(nc.vector.tensor_scalar(coef[:, 0:BC], rn[:], w_l[:], None, ALU.mult), 1)
                    diagonals(1, 1)
                    gaussian_bias(1)
                    split_diag(1, slice(NC, BC), 3, diag_ready, 2 * BC * u + 2 * BC)
                    v_low(0)
                    cosines(0)
                    v_low(1)
                    cosines(1)
                    gaussians(0)
                    v_low(2)
                    gaussians(1)
                    v_low(3)
                    dve.wait_ge(tl_ready, BC * u + BC)
                    coefs(nc.vector.tensor_tensor(deg[:, 0:BC], deg[:, 0:BC], rn[:], ALU.mult), 2)
                    dve.wait_ge(tg_ready, BC * u + BC)
                    coefs(nc.vector.tensor_scalar(dm[:], deg[:], DEG_EPS, None, ALU.max), 3)
                    coefs(nc.vector.reciprocal(drec[:], dm[:]), 4)
                    coefs(nc.vector.tensor_tensor(cnorm[:], drec[:], coef[:], ALU.mult), 5)
                    combine(0)
                    combine(1)
                    x_low(0)
                    x_low(1)
                    kt_low(0)
                    kt_low(1)
                    residual(0)
                    residual(1)
                    row_stats(0)
                    row_stats(1)
                    residual(2)
                    row_moments(0)
                    x_low(2)
                    residual(3)
                    x_low(3)
                    row_stats(2)
                    row_stats(3)
                    row_moments(1)

        @block.tensor
        def _(pe):
            def product(bank, lhs, rhs, ks, sem, start=True):
                n = 0
                for k in ks:
                    for l, r in PASSES:
                        ins = nc.tensor.matmul(bank, lhs(l, k), rhs(r, k), start=(start and n == 0),
                                               stop=(n == 3 * len(ks) - 1), skip_group_check=not start)
                        n += 1
                ins.then_inc(sem, 1)

            def transpose_x(t, bank):
                for i in range(BC):
                    ins = nc.tensor.transpose(ring[:, bank, i * P:(i + 1) * P], x_tr[:, i, t * P:(t + 1) * P], ident[:])
                ins.then_inc(ring_full, 1)

            pe.wait_ge(xtr_loaded, 16)
            for t in range(ND):
                if t >= 2:
                    pe.wait_ge(lo_ready, t - 1)
                transpose_x(t, t % 2)
            with pe.Fori(0, LAYERS) as layer:
                pe.wait_ge(vo_loaded, 32 * layer + 32)
                for d in range(ND):
                    for f in range(ND):
                        ins = nc.tensor.matmul(gram[:, d // B, d % B].rearrange("p c f -> p (c f)"),
                                               stage_a[:, f, d * P:(d + 1) * P], stage_b[:, f],
                                               start=(f == 0), stop=(f == ND - 1))
                ins.then_inc(wvo_full, 1)
                with pe.Fori(0, PAIRS) as pair:
                    u = layer * PAIRS + pair
                    for i in range(2 * ND):
                        e = i % ND
                        w = wz2[i // ND]
                        if i == 0:
                            pe.wait_ge(w_lo, 3 * layer + 3)
                            pe.wait_ge(s_ready, BC * u)
                            pe.wait_ge(lo_ready, splits(u, 0))
                        elif i >= 2:
                            pe.wait_ge(lo_ready, splits(u, i - 1))
                        product(ring[:, i % 2], lambda h, k: w[:, h, k, e * P:(e + 1) * P],
                                lambda h, k: xT2[:, h, k], range(ND), ring_full)
                    for g in range(2):
                        pe.wait_ge(lo_ready, splits(u, ND * (g + 1)))
                        for b in range(B):
                            n = 0
                            for c in range(NC):
                                rows = slice(b * C + c * P, b * C + (c + 1) * P)
                                for k in range(ND):
                                    for l, r in PASSES:
                                        ins = nc.tensor.matmul(
                                            gram[:, g, b, c], z2[g][:, l, k, rows], z2[g][:, r, k, b * C:(b + 1) * C],
                                            start=(n == 0), stop=(n == 2 * 3 * ND - 1), skip_group_check=True)
                                        n += 1
                            ins.then_inc(gram_full, 1)

                    def v(i):
                        pe.wait_ge(lo_ready, splits(u, V0 + i - 1))
                        product(ring[:, i % 2], lambda h, k: xT2[:, h, k, i * P:(i + 1) * P],
                                lambda h, k: wvo2[:, h, k], range(ND), ring_full)

                    def column_norms():
                        pe.wait_ge(dlo_ready, (B + 1) * u + 2)
                        for h in (HI, LO):
                            ins = nc.tensor.matmul(rbank[:].rearrange("p b f -> p (b f)"), ones_r[:],
                                                   diag2[:, 0, h].rearrange("p i f -> p (i f)"),
                                                   start=(h == HI), stop=(h == LO))
                        ins.then_inc(r_full, 1)

                    def add_squares(b):
                        pe.wait_ge(dlo_ready, (B + 1) * u + (1, 3)[b])
                        for c in range(NC):
                            for h in (HI, LO):
                                ins = nc.tensor.matmul(
                                    gram[:, 1, b, c], ones_r[:],
                                    diag2[:, 1, h, NC * b:NC * (b + 1)].rearrange("p i f -> p (i f)"),
                                    start=False, stop=(c == NC - 1 and h == LO), skip_group_check=True)
                        ins.then_inc(sq_added, 1)

                    v(0)
                    column_norms()
                    add_squares(0)
                    v(1)
                    add_squares(1)
                    v(2)
                    v(3)

                    def transposed_k(b):
                        pe.wait_ge(k_ready, BC * u + NC * (b + 1))
                        pe.wait_ge(kt_lo, B * u + b)
                        for m in range(NC):
                            for c in range(NC):
                                ins = nc.tensor.transpose(tbank[:, m, c * P:(c + 1) * P],
                                                          km[:, NC * b + c, m * P:(m + 1) * P], ident[:])
                        ins.then_inc(kt_full, 1)

                    def x_chunk(t):
                        if t == 0:
                            pe.wait_ge(xtr_loaded, 16 * u + 32)
                        transpose_x(t, tail_at(f"t{t}") % 2)

                    def kv(i):
                        b, c = i // NC, i % NC
                        product(ring[:, tail_at(f"k{i}") % 2], lambda h, m: kT2[:, h, b, m, c * P:(c + 1) * P],
                                lambda h, m: v2[:, h, NC * b + m], range(NC), ring_full)

                    pe.wait_ge(lo_ready, splits(u, T0 - 1))
                    x_chunk(0)
                    pe.wait_ge(lo_ready, splits(u, T0))
                    x_chunk(1)
                    transposed_k(0)
                    transposed_k(1)
                    pe.wait_ge(lo_ready, splits(u, T0 + 1))
                    kv(0)
                    pe.wait_ge(lo_ready, splits(u, T0 + 2))
                    kv(1)
                    pe.wait_ge(kt_lo, B * u + 2)
                    pe.wait_ge(s_ready, BC * u + 1)
                    kv(2)
                    pe.wait_ge(s_ready, BC * u + 2)
                    x_chunk(2)
                    pe.wait_ge(s_ready, BC * u + 3)
                    kv(3)
                    pe.wait_ge(lo_ready, splits(u, T0 + 3))
                    x_chunk(3)


def build(nc, x, adj, adjT, columns, bias, wlT, wgT, wv, woT, gate, log_sigma, out):
    with ExitStack() as ctx:
        ident = ctx.enter_context(nc.sbuf_tensor("ident", [P, P], F32))
        ones = ctx.enter_context(nc.sbuf_tensor("ones", [P, P], F32))
        ones_r = ctx.enter_context(nc.sbuf_tensor("ones_r", [P, P], F32R))
        ident_zero = ctx.enter_context(nc.semaphore("ident_zero"))
        ones_done = ctx.enter_context(nc.semaphore("ones_done"))
        with nc.Block() as block:
            @block.gpsimd
            def _(pool):
                nc.gpsimd.memset(ident[:], 0.0).then_inc(ident_zero, 1)
                pool.wait_ge(ident_zero, 1)
                nc.gpsimd.affine_select(out=ident[:], in_=ident[:], compare_op=ALU.not_equal, fill=1.0, base=0,
                                        pattern=[[-1, P]], channel_multiplier=1)

            @block.vector
            def _(dve):
                nc.vector.memset(ones[:], 1.0).then_inc(ones_done, 1)
                dve.wait_ge(ones_done, 1)
                nc.vector.tensor_copy(ones_r[:], ones[:])

        setup = {"ident": ident, "ones": ones, "ones_r": ones_r}
        attention_and_hop(nc, setup, x, adj, adjT, columns, bias, out)
        kernel_similarity_layers(nc, setup, adj, wlT, wgT, wv, woT, gate, log_sigma, out)


def kernel(**inputs):
    import numpy as np
    import concourse.bacc as bacc
    from concourse.bass_utils import run_bass_kernel_spmd as run

    def layers(name, turn):
        both = [np.asarray(inputs[f"L{i}_gnn_{name}"]) for i in (2, 3)]
        return np.ascontiguousarray(np.stack([w.T if turn else w for w in both]))

    def columns(*names):
        return np.ascontiguousarray(np.stack([np.asarray(inputs[n]).reshape(-1, P).T for n in names], axis=1))

    arrays = {
        "x": np.asarray(inputs["x"]),
        "adj": np.asarray(inputs["adj"]),
        "adjT": np.ascontiguousarray(np.asarray(inputs["adj"]).T),
        "columns": columns("L0_gnn_wq", "L0_gnn_wk", "L0_gnn_bm"),
        "bias": np.asarray(inputs["L1_gnn_bias"]),
        "wlT": layers("W_lang", True),
        "wgT": layers("W_grav", True),
        "wv": layers("W_V", False),
        "woT": layers("W_O", True),
        "gate": layers("gate_logit", False),
        "log_sigma": layers("log_sigma", False),
    }
    nc = bacc.Bacc("TRN2", target_bir_lowering=False, num_devices=1)
    args = [nc.dram_tensor(f"in_{k}", a.shape, mybir.dt.from_np(a.dtype), kind="ExternalInput").ap()
            for k, a in arrays.items()]
    out = nc.dram_tensor("out_x", arrays["x"].shape, F32, kind="ExternalOutput").ap()
    build(nc, *args, out)
    r = run(nc, [{f"in_{k}": a for k, a in arrays.items()}], core_ids=[0])
    return r.results[0]["out_x"]
```

```python
from contextlib import ExitStack

import concourse.bass as bass
from concourse import mybir

F32 = mybir.dt.float32
F32R = mybir.dt.float32r
ALU = mybir.AluOpType
ACT = mybir.ActivationFunctionType
AX = mybir.AxisListType

P = 128
LN_EPS = 1e-5
DEG_EPS = 1e-8
SLOPE = 0.01

HI, LO = 0, 1
PASSES = ((HI, HI), (LO, HI), (HI, LO))


def attention_and_hop(nc, setup, x, adj, adjT, columns, bm, bias, out):
    BATCH, C, N = x.shape
    NC, NN = C // P, N // P
    YW = C + 2
    ident, ones = setup["ident"], setup["ones"]
    E_POOL = NN - 1

    with ExitStack() as ctx:
        def sb(name, shape, dt=F32):
            return ctx.enter_context(nc.sbuf_tensor("a_" + name, shape, dt))

        def ps(name, shape):
            return ctx.enter_context(nc.psum_tensor("a_" + name, shape, F32))

        def sem(name):
            return ctx.enter_context(nc.semaphore("a_" + name))

        adjq = sb("adjq", [P, NC, YW])
        adjq2 = sb("adjq2", [P, 2, NC, YW], F32R)
        adjn = sb("adjn", [P, NC, C])
        hop = sb("hop", [P, NC, C])
        hop2 = sb("hop2", [P, 2, NC, C], F32R)
        cols = sb("cols", [P, 2, NC])
        wkb = sb("wkb", [P, NC, P])
        wkb2 = sb("wkb2", [P, 2, NC, P], F32R)
        bmb = sb("bmb", [P, C])
        biasb = sb("biasb", [P, N])
        nhalf = sb("nhalf", [P, NC])
        spare = sb("spare", [P, 1])

        x_in = sb("x_in", [P, NC, N])
        x2 = sb("x2", [P, 2, NC, N], F32R)
        x_res = sb("x_res", [P, NC, N])
        y2 = [sb(f"y2_{i}", [P, 2, NN, YW], F32R) for i in range(2)]
        e2 = [sb(f"e2_{i}", [P, 2, NN, N], F32R) for i in range(2)]
        qcol = sb("qcol", [P, NN])
        qtop = sb("qtop", [P, 1])
        qdiag = sb("qdiag", [P, P])
        qmax = sb("qmax", [P, 1])
        qs = sb("qs", [P, NN])
        ea = sb("ea", [P, NN])
        eb = sb("eb", [P, NN])
        karg = sb("karg", [P, 2, N])
        kexp = sb("kexp", [P, 2, N])
        e1 = sb("e1", [P, 2, N])
        e = sb("e", [P, NN, N])
        rden = sb("rden", [P, NN])
        oT = sb("oT", [P, NN, C])
        s0 = sb("s0", [P, NC, N])
        stats = sb("stats", [P, 2, NC, 6])
        mv = sb("mv", [P, 2, NC, 2])
        ve = sb("ve", [P, 2, NC])
        rstd = sb("rstd", [P, 2, NC])
        nmean = sb("nmean", [P, 2, NC])
        nmr = sb("nmr", [P, 2, NC])
        x1 = sb("x1", [P, NC, N])
        x12 = sb("x12", [P, 2, NC, N], F32R)
        xb = sb("xb", [P, NC, N])
        s1 = sb("s1", [P, NC, N])
        yout = sb("yout", [P, NC, N])

        BANK = 512
        agg = ps("agg", [P, NN, BANK])
        kbank = ps("kbank", [P, N])
        ring = ps("ring", [P, 2, BANK])
        qbank = ps("qbank", [P, P])

        const_loaded = sem("const_loaded")
        const_step = sem("const_step")
        adjq_ready = sem("adjq_ready")
        wk_ready = sem("wk_ready")
        hop_ready = sem("hop_ready")
        nhalf_ready = sem("nhalf_ready")
        ones_ready = sem("ones_ready")
        x_loaded = sem("x_loaded")
        xres_loaded = sem("xres_loaded")
        x_hi = sem("x_hi")
        x_lo = sem("x_lo")
        y_full = sem("y_full")
        y_hi = sem("y_hi")
        y_lo = sem("y_lo")
        q_copied = sem("q_copied")
        q_step = sem("q_step")
        k_full = sem("k_full")
        q_full = sem("q_full")
        karg_ready = sem("karg_ready")
        kexp_ready = sem("kexp_ready")
        qexp_ready = sem("qexp_ready")
        e1_ready = sem("e1_ready")
        e_ready = sem("e_ready")
        e_hi = sem("e_hi")
        e_lo_pool = sem("e_lo_pool")
        e_lo_dve = sem("e_lo_dve")
        agg_full = sem("agg_full")
        rden_ready = sem("rden_ready")
        oT_ready = sem("oT_ready")
        o_full = sem("o_full")
        s0_ready = sem("s0_ready")
        stats_ready = sem("stats_ready")
        mv_ready = sem("mv_ready")
        ve_ready = sem("ve_ready")
        ln_step = sem("ln_step")
        x1_ready = sem("x1_ready")
        x1_hi = sem("x1_hi")
        x1_lo = sem("x1_lo")
        xb_ready = sem("xb_ready")
        hop_full = sem("hop_full")
        s1_ready = sem("s1_ready")
        y_ready = sem("y_ready")
        y_stored = sem("y_stored")

        def nodes(ap):
            return ap.rearrange("(c p) f -> p c f", p=P)

        def turns(engine, turn):
            turn(0, 0, False, False, True, True)
            turn(1, 1, True, False, True, True)
            with engine.Fori(1, BATCH // 2 - 1) as half:
                turn(2 * half, 0, True, True, True, True)
                turn(2 * half + 1, 1, True, True, True, True)
            turn(BATCH - 2, 0, True, True, True, False)
            turn(BATCH - 1, 1, True, True, False, False)

        block = ctx.enter_context(nc.Block())

        @block.sync
        def _(sp):
            def load_x(m):
                sp.dma_start(x_in[:], nodes(x[m])).then_inc(x_loaded, 16)

            def load_residual(n):
                sp.wait_ge(s0_ready, NC * n)
                sp.dma_start(x_res[:], nodes(x[n])).then_inc(xres_loaded, 16)

            def store(n):
                sp.wait_ge(y_ready, NC * n + NC)
                sp.dma_start(nodes(out[n]), yout[:]).then_inc(y_stored, 16)

            load_x(0)
            sp.dma_start(adjq[:, :, 0:C], nodes(adjT)).then_inc(const_loaded, 16)
            sp.dma_start(cols[:], columns).then_inc(const_loaded, 16)
            sp.dma_start(adjn[:], nodes(adj)).then_inc(const_loaded, 16)
            sp.dma_start(bmb[:], bm.partition_broadcast(P)).then_inc(const_loaded, 16)
            sp.dma_start(biasb[:], bias.partition_broadcast(P)).then_inc(const_loaded, 16)
            for m in (1, 2):
                sp.wait_ge(x_lo, m)
                load_x(m)
            for n in (0, 1):
                load_residual(n)
                sp.wait_ge(x_lo, n + 3)
                load_x(n + 3)
            with sp.Fori(2, BATCH - 3) as n:
                load_residual(n)
                store(n - 2)
                sp.wait_ge(x_lo, n + 3)
                load_x(n + 3)
            for n in range(BATCH - 3, BATCH):
                load_residual(n)
                store(n - 2)
            store(BATCH - 2)
            store(BATCH - 1)
            sp.wait_ge(y_stored, 16 * BATCH)

        @block.gpsimd
        def _(pool):
            nc.gpsimd.memset(nhalf[:], -0.5).then_inc(nhalf_ready, 1)
            pool.wait_ge(nhalf_ready, 1)
            for i in range(2):
                nc.gpsimd.memset(y2[i][:, HI, :, C:YW].bitcast(F32), 1.0).then_inc(ones_ready, 1)
                nc.gpsimd.memset(y2[i][:, LO, :, C:YW].bitcast(F32), 0.0).then_inc(ones_ready, 1)

            def split_x(m):
                pool.wait_ge(x_hi, m + 1)
                nc.gpsimd.tensor_tensor(x2[:, LO], x_in[:], x2[:, HI].bitcast(F32), ALU.subtract).then_inc(x_lo, 1)

            def e_low(m, par):
                for c in range(E_POOL):
                    pool.wait_ge(e_hi, NN * m + c + 1)
                    nc.gpsimd.tensor_tensor(e2[par][:, LO, c], e[:, c], e2[par][:, HI, c].bitcast(F32),
                                            ALU.subtract).then_inc(e_lo_pool, 1)

            def norm_scalars(which, m, nth):
                pool.wait_ge(ve_ready, 2 * nth + 2)
                nc.gpsimd.tensor_tensor(rstd[:, which], ve[:, which], nhalf[:], ALU.pow).then_inc(ln_step, 1)
                pool.wait_ge(ln_step, 2 * nth + 1)
                nc.gpsimd.tensor_tensor(nmr[:, which], nmean[:, which], rstd[:, which], ALU.mult).then_inc(ln_step, 1)

            def biased(m):
                for c in range(NC):
                    pool.wait_ge(x1_ready, NC * m + c + 1)
                    nc.gpsimd.tensor_tensor(xb[:, c], x1[:, c], biasb[:], ALU.add).then_inc(xb_ready, 1)

            def turn(n, par, before, earlier, coming, later):
                if before:
                    norm_scalars(0, n - 1, 2 * (n - 1))
                    biased(n - 1)
                if later:
                    split_x(n + 2)
                if coming:
                    e_low(n + 1, 1 - par)
                if before:
                    norm_scalars(1, n - 1, 2 * (n - 1) + 1)

            split_x(0)
            split_x(1)
            e_low(0, 0)
            pool.wait_ge(const_loaded, 16 * 5)
            turns(pool, turn)
            norm_scalars(0, BATCH - 1, 2 * (BATCH - 1))
            biased(BATCH - 1)
            norm_scalars(1, BATCH - 1, 2 * (BATCH - 1) + 1)

        @block.scalar
        def _(act):
            def x_high(m):
                act.wait_ge(x_loaded, 16 * m + 16)
                act.wait_ge(k_full, m)
                nc.scalar.activation(x2[:, HI], x_in[:], ACT.Copy).then_inc(x_hi, 1)

            def y_high(m, par):
                for c in range(NN):
                    act.wait_ge(y_full, NN * m + c + 1)
                    nc.scalar.activation(y2[par][:, HI, c, 0:C], ring[:, c % 2, 0:C], ACT.Copy).then_inc(y_hi, 1)

            def exponentials(m):
                act.wait_ge(q_step, 5 * m + 4)
                nc.scalar.activation(ea[:], qs[:], ACT.Exp).then_inc(qexp_ready, 1)
                nc.scalar.activation(eb[:], qs[:], ACT.Exp, scale=SLOPE).then_inc(qexp_ready, 1)
                for i, scale in ((0, 1.0 - SLOPE), (1, SLOPE - 1.0)):
                    act.wait_ge(karg_ready, 2 * m + i + 1)
                    nc.scalar.activation(kexp[:, i], karg[:, i], ACT.Exp, scale=scale).then_inc(kexp_ready, 1)

            def e_first(m, c):
                if c == 0:
                    act.wait_ge(kexp_ready, 2 * m + 1)
                    act.wait_ge(qexp_ready, 2 * m + 2)
                nc.scalar.activation(e1[:, c % 2], kexp[:, 0], ACT.Copy, scale=ea[:, c:c + 1]).then_inc(e1_ready, 1)

            def e_high(m, par, c):
                act.wait_ge(e_ready, NN * m + c + 1)
                nc.scalar.activation(e2[par][:, HI, c], e[:, c], ACT.Copy).then_inc(e_hi, 1)

            def e_chunks(m, par):
                e_first(m, 0)
                e_first(m, 1)
                for c in range(2, NN):
                    e_high(m, par, c - 2)
                    e_first(m, c)
                e_high(m, par, NN - 2)
                e_high(m, par, NN - 1)

            def first_norm(m):
                act.wait_ge(ln_step, 4 * m + 2)
                for c in range(NC):
                    nc.scalar.activation(x1[:, c], s0[:, c], ACT.Identity, bias=nmr[:, 0, c:c + 1],
                                         scale=rstd[:, 0, c:c + 1]).then_inc(x1_ready, 1)
                act.wait_ge(hop_full, NC * m)
                for c in range(NC):
                    nc.scalar.activation(x12[:, HI, c], s0[:, c], ACT.Identity, bias=nmr[:, 0, c:c + 1],
                                         scale=rstd[:, 0, c:c + 1]).then_inc(x1_hi, 1)

            def second_norm(m):
                act.wait_ge(ln_step, 4 * m + 4)
                act.wait_ge(y_stored, 16 * m)
                for c in range(NC):
                    nc.scalar.activation(yout[:, c], s1[:, c], ACT.Identity, bias=nmr[:, 1, c:c + 1],
                                         scale=rstd[:, 1, c:c + 1]).then_inc(y_ready, 1)

            def turn(n, par, before, earlier, coming, later):
                if coming:
                    y_high(n + 1, 1 - par)
                if earlier:
                    second_norm(n - 2)
                if before:
                    first_norm(n - 1)
                if later:
                    x_high(n + 2)
                if coming:
                    exponentials(n + 1)
                    e_chunks(n + 1, 1 - par)

            x_high(0)
            y_high(0, 0)
            x_high(1)
            exponentials(0)
            e_chunks(0, 0)
            turns(act, turn)
            second_norm(BATCH - 2)
            first_norm(BATCH - 1)
            second_norm(BATCH - 1)

        @block.vector
        def _(dve):
            steps = [0]

            def step(ins):
                steps[0] += 1
                ins.then_inc(const_step, 1)
                dve.wait_ge(const_step, steps[0])

            step(nc.vector.memset(adjq[:, :, C + 1:C + 2], 0.0))
            dve.wait_ge(const_loaded, 16 * 5)
            step(nc.vector.tensor_copy(adjq[:, :, C], cols[:, 0]))
            step(nc.vector.tensor_copy(adjq2[:, HI], adjq[:]))
            nc.vector.tensor_tensor(adjq2[:, LO], adjq[:], adjq2[:, HI].bitcast(F32),
                                    ALU.subtract).then_inc(adjq_ready, 1)
            for c in range(NC):
                step(nc.vector.tensor_scalar(wkb[:, c], ones[:], cols[:, 1, c:c + 1], None, ALU.mult))
            step(nc.vector.tensor_copy(wkb2[:, HI], wkb[:]))
            nc.vector.tensor_tensor(wkb2[:, LO], wkb[:], wkb2[:, HI].bitcast(F32), ALU.subtract).then_inc(wk_ready, 1)
            step(nc.vector.tensor_tensor(hop[:], adjn[:], adjn[:], ALU.mult))
            step(nc.vector.tensor_copy(hop2[:, HI], hop[:]))
            nc.vector.tensor_tensor(hop2[:, LO], hop[:], hop2[:, HI].bitcast(F32), ALU.subtract).then_inc(hop_ready, 1)

            def y_low(m, par, c):
                dve.wait_ge(y_hi, NN * m + c + 1)
                nc.vector.tensor_copy(qcol[:, c:c + 1], ring[:, c % 2, C:C + 1]).then_inc(q_copied, 1)
                nc.vector.tensor_tensor(y2[par][:, LO, c, 0:C], ring[:, c % 2, 0:C],
                                        y2[par][:, HI, c, 0:C].bitcast(F32), ALU.subtract).then_inc(y_lo, 1)

            def q_diagonal(m):
                dve.wait_ge(q_copied, NN * m + NN)
                nc.vector.tensor_reduce(qtop[:], qcol[:], AX.X, ALU.max).then_inc(q_step, 1)
                dve.wait_ge(q_step, 5 * m + 1)
                nc.vector.tensor_scalar(qdiag[:], ident[:], qtop[:], None, ALU.mult).then_inc(q_step, 1)

            def q_and_k(m):
                dve.wait_ge(q_full, m + 1)
                nc.vector.tensor_reduce(qmax[:], qbank[:], AX.X, ALU.max).then_inc(q_step, 1)
                dve.wait_ge(q_step, 5 * m + 3)
                nc.vector.tensor_scalar(qs[:], qcol[:], qmax[:], None, ALU.subtract).then_inc(q_step, 1)
                dve.wait_ge(k_full, m + 1)
                dve.wait_ge(kexp_ready, 2 * m)
                nc.vector.tensor_scalar(karg[:, 0], kbank[:], qmax[:], 0.0, ALU.add, ALU.min).then_inc(karg_ready, 1)
                nc.vector.tensor_scalar(karg[:, 1], kbank[:], qmax[:], 0.0, ALU.add, ALU.max).then_inc(karg_ready, 1)
                nc.vector.memset(spare[:], 0.0).then_inc(q_step, 1)

            def e_max(m, c):
                dve.wait_ge(e1_ready, NN * m + c + 1)
                if c == 0:
                    dve.wait_ge(kexp_ready, 2 * m + 2)
                if c < E_POOL:
                    dve.wait_ge(e_lo_pool, E_POOL * m)
                nc.vector.scalar_tensor_tensor(out=e[:, c], in0=kexp[:, 1], scalar=eb[:, c:c + 1],
                                               in1=e1[:, c % 2], op0=ALU.mult, op1=ALU.max).then_inc(e_ready, 1)

            def e_low(m, par):
                dve.wait_ge(e_hi, NN * m + NN)
                nc.vector.tensor_tensor(e2[par][:, LO, NN - 1], e[:, NN - 1], e2[par][:, HI, NN - 1].bitcast(F32),
                                        ALU.subtract).then_inc(e_lo_dve, 1)

            def outputs(n):
                dve.wait_ge(agg_full, n + 1)
                nc.vector.reciprocal(rden[:], agg[:, :, C]).then_inc(rden_ready, 1)
                dve.wait_ge(rden_ready, n + 1)
                for i in range(NN):
                    nc.vector.scalar_tensor_tensor(out=oT[:, i], in0=agg[:, i, 0:C], scalar=rden[:, i:i + 1],
                                                   in1=bmb[:], op0=ALU.mult, op1=ALU.add).then_inc(oT_ready, 1)

            def first_residual(m, c):
                dve.wait_ge(o_full, NC * m + c + 1)
                dve.wait_ge(xres_loaded, 16 * m + 16)
                nc.vector.scalar_tensor_tensor(out=s0[:, c], in0=ring[:, c % 2], scalar=0.0, in1=x_res[:, c],
                                               op0=ALU.max, op1=ALU.add).then_inc(s0_ready, 1)

            def second_residual(m, c):
                dve.wait_ge(hop_full, NC * m + c + 1)
                dve.wait_ge(xb_ready, NC * m + c + 1)
                if c == 0:
                    dve.wait_ge(y_ready, NC * m)
                nc.vector.tensor_tensor(s1[:, c], ring[:, c % 2], xb[:, c], ALU.add).then_inc(s1_ready, 1)

            def row_stats(which, m, c):
                dve.wait_ge((s0_ready, s1_ready)[which], NC * m + c + 1)
                nc.vector.bn_stats(stats[:, which, c], (s0, s1)[which][:, c]).then_inc(stats_ready, 1)

            def row_moments(which, m):
                nth = 2 * m + which + 1
                dve.wait_ge(stats_ready, NC * nth)
                nc.vector.memset(spare[:], 0.0)
                for c in range(NC):
                    nc.vector.bn_aggr(mv[:, which, c], stats[:, which, c]).then_inc(mv_ready, 1)
                dve.wait_ge(mv_ready, NC * nth)
                nc.vector.tensor_scalar(ve[:, which], mv[:, which, :, 1], LN_EPS, None, ALU.add).then_inc(ve_ready, 1)
                nc.vector.tensor_scalar(nmean[:, which], mv[:, which, :, 0], -1.0, None, ALU.mult).then_inc(ve_ready, 1)

            def x1_low(m):
                for c in range(NC):
                    dve.wait_ge(x1_hi, NC * m + c + 1)
                    nc.vector.tensor_tensor(x12[:, LO, c], x1[:, c], x12[:, HI, c].bitcast(F32),
                                            ALU.subtract).then_inc(x1_lo, 1)

            def turn(n, par, before, earlier, coming, later):
                if before:
                    first_residual(n - 1, 0)
                    first_residual(n - 1, 1)
                    row_stats(0, n - 1, 0)
                if coming:
                    y_low(n + 1, 1 - par, 0)
                if before:
                    row_stats(0, n - 1, 1)
                if coming:
                    y_low(n + 1, 1 - par, 1)
                if before:
                    row_moments(0, n - 1)
                if coming:
                    y_low(n + 1, 1 - par, 2)
                    y_low(n + 1, 1 - par, 3)
                    q_diagonal(n + 1)
                if before:
                    x1_low(n - 1)
                if coming:
                    q_and_k(n + 1)
                    for c in range(NN):
                        e_max(n + 1, c)
                outputs(n)
                if coming:
                    e_low(n + 1, 1 - par)
                if before:
                    for c in range(NC):
                        second_residual(n - 1, c)
                        row_stats(1, n - 1, c)
                    row_moments(1, n - 1)

            for c in range(NN):
                y_low(0, 0, c)
            q_diagonal(0)
            q_and_k(0)
            for c in range(NN):
                e_max(0, c)
            e_low(0, 0)
            turns(dve, turn)
            for c in range(NC):
                first_residual(BATCH - 1, c)
                row_stats(0, BATCH - 1, c)
            row_moments(0, BATCH - 1)
            x1_low(BATCH - 1)
            for c in range(NC):
                second_residual(BATCH - 1, c)
                row_stats(1, BATCH - 1, c)
            row_moments(1, BATCH - 1)

        @block.tensor
        def _(pe):
            def y_chunks(m, before):
                pe.wait_ge(x_lo, m + 1)
                for c in range(NN):
                    if c >= 2:
                        pe.wait_ge(y_lo, NN * m + c - 1)
                    elif before:
                        pe.wait_ge(s0_ready, NC * (m - 2) + c + 1)
                    else:
                        pe.wait_ge(y_lo, NN * m)
                    mm = 0
                    for l, r in PASSES:
                        for k in range(NC):
                            ins = nc.tensor.matmul(ring[:, c % 2, 0:YW], x2[:, l, k, c * P:(c + 1) * P],
                                                   adjq2[:, r, k], start=(mm == 0), stop=(mm == 3 * NC - 1))
                            mm += 1
                    ins.then_inc(y_full, 1)

            def keys(m):
                pe.wait_ge(karg_ready, 2 * m)
                mm = 0
                for l, r in PASSES:
                    for k in range(NC):
                        ins = nc.tensor.matmul(kbank[:], wkb2[:, l, k], x2[:, r, k],
                                               start=(mm == 0), stop=(mm == 3 * NC - 1))
                        mm += 1
                ins.then_inc(k_full, 1)

            def spread_q(m):
                pe.wait_ge(q_step, 5 * m + 2)
                nc.tensor.matmul(qbank[:], ones[:], qdiag[:], start=True, stop=True).then_inc(q_full, 1)

            def attention(n, par, c):
                pe.wait_ge(e_hi, NN * n + c + 1)
                if c < E_POOL:
                    pe.wait_ge(e_lo_pool, E_POOL * n + c + 1)
                else:
                    pe.wait_ge(e_lo_dve, n + 1)
                for i in range(NN):
                    for l, r in PASSES:
                        ins = nc.tensor.matmul(agg[:, i, 0:YW], e2[par][:, l, c, i * P:(i + 1) * P], y2[par][:, r, c],
                                               start=(c == 0 and (l, r) == PASSES[0]),
                                               stop=(c == NN - 1 and (l, r) == PASSES[-1]))
                if c == NN - 1:
                    ins.then_inc(agg_full, 1)

            def turn_outputs(m):
                pe.wait_ge(s1_ready, NC * m)
                pe.wait_ge(oT_ready, NN * m + NN)
                for c in range(NC):
                    for i in range(NN):
                        ins = nc.tensor.transpose(ring[:, c % 2, i * P:(i + 1) * P], oT[:, i, c * P:(c + 1) * P],
                                                  ident[:])
                    ins.then_inc(o_full, 1)

            def hops(m, coming):
                for i in range(NC):
                    if coming:
                        pe.wait_ge(y_lo, NN * (m + 2) + NN - NC + i + 1)
                    else:
                        pe.wait_ge(s0_ready, NC * m + i + 1)
                    mm = 0
                    for k in range(NC):
                        if i == 0:
                            pe.wait_ge(x1_lo, NC * m + k + 1)
                        for l, r in PASSES:
                            ins = nc.tensor.matmul(ring[:, i % 2], hop2[:, l, k, i * P:(i + 1) * P], x12[:, r, k],
                                                   start=(mm == 0), stop=(mm == 3 * NC - 1))
                            mm += 1
                    ins.then_inc(hop_full, 1)

            def turn(n, par, before, earlier, coming, later):
                if before:
                    pe.wait_ge(y_lo, NN * n + NN)
                    turn_outputs(n - 1)
                if coming:
                    y_chunks(n + 1, before)
                    keys(n + 1)
                attention(n, par, 0)
                if coming:
                    spread_q(n + 1)
                for c in range(1, NN):
                    attention(n, par, c)
                if before:
                    hops(n - 1, coming)

            pe.wait_ge(adjq_ready, 1)
            y_chunks(0, False)
            pe.wait_ge(wk_ready, 1)
            keys(0)
            spread_q(0)
            pe.wait_ge(hop_ready, 1)
            pe.wait_ge(ones_ready, 4)
            turns(pe, turn)
            turn_outputs(BATCH - 1)
            hops(BATCH - 1, False)


def kernel_similarity_layers(nc, setup, adj, wlT, wgT, wv, woT, gate, log_sigma, out):
    LAYERS = wlT.shape[0]
    BATCH, C, D = out.shape
    B = 2
    NC, ND = C // P, D // P
    PAIRS = BATCH // B
    ROWS = B * C
    BC = B * NC
    ident, ones_r = setup["ident"], setup["ones_r"]

    with ExitStack() as ctx:
        def sb(name, shape, dt=F32):
            return ctx.enter_context(nc.sbuf_tensor("l_" + name, shape, dt))

        def ps(name, shape):
            return ctx.enter_context(nc.psum_tensor("l_" + name, shape, F32))

        def sem(name):
            return ctx.enter_context(nc.semaphore("l_" + name))

        stage_a = sb("stage_a", [P, ND, D])
        stage_b = sb("stage_b", [P, ND, D])
        wz2 = [sb("wl2", [P, 2, ND, D], F32R), sb("wg2", [P, 2, ND, D], F32R)]
        wvo2 = sb("wvo2", [P, 2, ND, D], F32R)
        adj_off = sb("adj_off", [P, NC, C])
        gate_in = sb("gate_in", [P, LAYERS])
        sigma_in = sb("sigma_in", [P, LAYERS])
        small = sb("small", [P, 8])
        spare = sb("spare", [P, 1])
        inv_s2 = sb("inv_s2", [P, 1])
        w_l = sb("w_l", [P, 1])
        expo = sb("expo", [P, BC])

        x_tr = sb("x_tr", [P, BC, D])
        x_res = sb("x_res", [P, BC, D])
        xT2 = sb("xT2", [P, 2, ND, ROWS], F32R)
        z2 = [sb("zl2", [P, 2, ND, ROWS], F32R), sb("zg2", [P, 2, ND, ROWS], F32R)]
        v2 = sb("v2", [P, 2, BC, D], F32R)
        sq = sb("sq", [P, 2, BC])
        sqm = sb("sqm", [P, BC])
        rn = sb("rn", [P, BC])
        gbias = sb("gbias", [P, BC])
        diag = sb("diag", [P, 2, BC, P])
        diag2 = sb("diag2", [P, 2, 2, BC, P], F32R)
        adj_r = sb("adj_r", [P, B, NC, C])
        e_g = sb("e_g", [P, BC, C])
        t_l = sb("t_l", [P, BC, C])
        t_g = sb("t_g", [P, BC, C])
        deg = sb("deg", [P, 2 * BC])
        dm = sb("dm", [P, 2 * BC])
        drec = sb("drec", [P, 2 * BC])
        coef = sb("coef", [P, 2 * BC])
        cnorm = sb("cnorm", [P, 2 * BC])
        km = sb("km", [P, BC, C])
        kT2 = sb("kT2", [P, 2, B, NC, C], F32R)
        s = sb("s", [P, BC, D])
        stats = sb("stats", [P, BC, 6])
        mv = sb("mv", [P, BC, 2])
        ve = sb("ve", [P, BC])
        rstd = sb("rstd", [P, BC])
        nmean = sb("nmean", [P, BC])
        nmr = sb("nmr", [P, BC])

        ring = ps("ring", [P, 2, 512])
        gram = ps("gram", [P, 2, B, NC, C])
        rbank = ps("rbank", [P, B, C])
        tbank = ps("tbank", [P, NC, C])

        consts_loaded = sem("consts_loaded")
        const_step = sem("const_step")
        expo_ready = sem("expo_ready")
        vo_loaded = sem("vo_loaded")
        z_loaded = sem("z_loaded")
        wvo_full = sem("wvo_full")
        w_hi = sem("w_hi")
        w_lo = sem("w_lo")
        scalar_exp = sem("scalar_exp")
        scalar_step = sem("scalar_step")
        coef_ready = sem("coef_ready")
        xtr_loaded = sem("xtr_loaded")
        xres_loaded = sem("xres_loaded")
        ring_full = sem("ring_full")
        hi_ready = sem("hi_ready")
        lo_ready = sem("lo_ready")
        gram_full = sem("gram_full")
        diag_ready = sem("diag_ready")
        sqm_ready = sem("sqm_ready")
        rn_ready = sem("rn_ready")
        gbias_ready = sem("gbias_ready")
        dl_ready = sem("dl_ready")
        dhi_ready = sem("dhi_ready")
        dlo_ready = sem("dlo_ready")
        r_full = sem("r_full")
        sq_added = sem("sq_added")
        adjr_ready = sem("adjr_ready")
        tl_ready = sem("tl_ready")
        eg_ready = sem("eg_ready")
        tg_ready = sem("tg_ready")
        coef_step = sem("coef_step")
        ve_ready = sem("ve_ready")
        scaled = sem("scaled")
        k_ready = sem("k_ready")
        kt_full = sem("kt_full")
        kt_hi = sem("kt_hi")
        kt_lo = sem("kt_lo")
        s_ready = sem("s_ready")
        stats_ready = sem("stats_ready")
        mv_ready = sem("mv_ready")
        ln_step = sem("ln_step")
        y_ready = sem("y_ready")
        y_stored = sem("y_stored")

        def weight(w):
            return w.rearrange("(k p) e -> p k e", p=P)

        def pair_rows(pair):
            return out.rearrange("(g b) (c p) f -> g p (b c) f", b=B, p=P)[pair]

        FIRST = ("l0", "l1", "l2", "l3", "g0", "g1", "g2", "g3", "v0", "v1", "v2", "v3")
        FULL = ("t0", "t1", "t2", "t3", "l0", "l1", "l2", "l3", "g0", "g1", "k0", "k1", "g2", "k2", "g3", "k3",
                "v0", "v1", "v2", "v3")
        SHORT = ("t0", "t1", "t2", "t3", "k0", "k1", "k2", "k3")

        class Order:

            def __init__(self, names, filled, split):
                self.names, self.filled, self.split = names, filled, split

            def bank(self, name):
                return self.names.index(name) % 2

            def fill(self, name):
                return self.filled + self.names.index(name) + 1

            def splits(self, name):
                return self.split + sum(n[0] != "k" for n in self.names[:self.names.index(name) + 1])

        def opening(layer):
            return Order(FIRST, ND + len(FULL) * PAIRS * layer, ND + (len(FULL) - BC) * PAIRS * layer)

        def turn(u, names):
            return Order(names, ND + len(FIRST) + len(FULL) * u, ND + len(FIRST) + (len(FULL) - BC) * u)

        block = ctx.enter_context(nc.Block())

        @block.sync
        def _(sp):
            sp.dma_start(adj_off[:], adj.rearrange("(c p) f -> p c f", p=P)).then_inc(consts_loaded, 16)
            sp.dma_start(gate_in[:], gate.partition_broadcast(P)).then_inc(consts_loaded, 16)
            sp.dma_start(sigma_in[:], log_sigma.partition_broadcast(P)).then_inc(consts_loaded, 16)
            sp.dma_start(x_tr[:], pair_rows(0)).then_inc(xtr_loaded, 16)
            sp.dma_start(stage_a[:], weight(wlT[0])).then_inc(z_loaded, 16)
            sp.dma_start(stage_b[:], weight(wgT[0])).then_inc(z_loaded, 16)
            sp.wait_ge(lo_ready, ND)
            sp.dma_start(x_tr[:], pair_rows(1)).then_inc(xtr_loaded, 16)
            for layer in range(LAYERS):
                sp.wait_ge(w_lo, 3 * layer + 2)
                sp.dma_start(stage_a[:], weight(wv[layer])).then_inc(vo_loaded, 16)
                sp.dma_start(stage_b[:], weight(woT[layer])).then_inc(vo_loaded, 16)
                if layer < LAYERS - 1:
                    sp.wait_ge(wvo_full, layer + 1)
                    sp.dma_start(stage_a[:], weight(wlT[layer + 1])).then_inc(z_loaded, 16)
                    sp.dma_start(stage_b[:], weight(wgT[layer + 1])).then_inc(z_loaded, 16)

                def step(u, pair, second):
                    sp.wait_ge(y_stored, 16 * B * u)
                    sp.dma_start(x_res[:], pair_rows(pair)).then_inc(xres_loaded, 16)
                    sp.wait_ge(lo_ready, turn(u, FULL).splits("t3"))
                    sp.dma_start(x_tr[:], pair_rows(second)).then_inc(xtr_loaded, 16)
                    for b in range(B):
                        sp.wait_ge(y_ready, BC * u + NC * (b + 1))
                        sp.dma_start(pair_rows(pair)[:, NC * b:NC * (b + 1)],
                                     s[:, NC * b:NC * (b + 1)]).then_inc(y_stored, 16)

                with sp.Fori(0, PAIRS - 2) as pair:
                    step(layer * PAIRS + pair, pair, pair + 2)
                for pair in (PAIRS - 2, PAIRS - 1):
                    step(layer * PAIRS + pair, pair, pair + 2 - PAIRS)
            sp.wait_ge(y_stored, 16 * B * LAYERS * PAIRS)
            sp.wait_ge(xtr_loaded, 16 * (LAYERS * PAIRS + 2))

        @block.gpsimd
        def _(pool):
            nc.gpsimd.memset(expo[:], -0.5).then_inc(expo_ready, 1)
            pool.wait_ge(expo_ready, 1)
            with pool.Fori(0, LAYERS) as layer:
                with pool.Fori(0, PAIRS) as pair:
                    u = layer * PAIRS + pair

                    pool.wait_ge(sqm_ready, u + 1)
                    nc.gpsimd.tensor_tensor(rn[:], sqm[:], expo[:, 0:BC], ALU.pow).then_inc(rn_ready, 1)
                    for b in range(B):
                        of = slice(NC * b, NC * (b + 1))
                        pool.wait_ge(ve_ready, 2 * (B * u + b) + 2)
                        nc.gpsimd.tensor_tensor(rstd[:, of], ve[:, of], expo[:, of], ALU.pow).then_inc(ln_step, 1)
                        pool.wait_ge(ln_step, 2 * (B * u + b) + 1)
                        nc.gpsimd.tensor_tensor(nmr[:, of], nmean[:, of], rstd[:, of], ALU.mult).then_inc(ln_step, 1)

        @block.scalar
        def _(act):
            def high(order, name):
                dst = {"t": xT2, "l": z2[0], "g": z2[1], "v": v2}[name[0]][:, HI, int(name[1])]
                act.wait_ge(ring_full, order.fill(name))
                nc.scalar.activation(dst, ring[:, order.bank(name)], ACT.Copy).then_inc(hi_ready, 1)

            for t in range(ND):
                high(Order(FULL, 0, 0), f"t{t}")
            with act.Fori(0, LAYERS) as layer:
                act.wait_ge(scalar_step, 6 * layer + 2)
                nc.scalar.activation(small[:, 2:3], small[:, 0:1], ACT.Exp, scale=-1.0).then_inc(scalar_exp, 1)
                nc.scalar.activation(inv_s2[:], small[:, 1:2], ACT.Exp, scale=-2.0).then_inc(scalar_exp, 1)
                for i, stage in enumerate((stage_a, stage_b)):
                    act.wait_ge(z_loaded, 32 * layer + 32)
                    nc.scalar.activation(wz2[i][:, HI], stage[:], ACT.Copy).then_inc(w_hi, 1)
                first = opening(layer)
                for name in FIRST[:2 * ND]:
                    high(first, name)
                act.wait_ge(wvo_full, layer + 1)
                nc.scalar.activation(wvo2[:, HI], gram[:].rearrange("p g b c f -> p (g b) (c f)"),
                                     ACT.Copy).then_inc(w_hi, 1)
                for name in FIRST[2 * ND:]:
                    high(first, name)

                def turn_of(u, names):
                    order = turn(u, names)

                    def coming(*wanted):
                        for name in wanted:
                            if name in names:
                                high(order, name)

                    def exps(b):
                        act.wait_ge(sq_added, B * u + b + 1)
                        act.wait_ge(gbias_ready, B * u + b + 1)
                        for c in range(NC):
                            i = NC * b + c
                            nc.scalar.activation(e_g[:, i], gram[:, 1, b, c], ACT.Exp, bias=gbias[:, i:i + 1],
                                                 scale=inv_s2[:]).then_inc(eg_ready, 1)

                    def kt_high(b):
                        act.wait_ge(kt_full, B * u + b + 1)
                        nc.scalar.activation(kT2[:, HI, b], tbank[:], ACT.Copy).then_inc(kt_hi, 1)

                    def normalise(b):
                        act.wait_ge(ln_step, 2 * (B * u + b) + 2)
                        for i in range(NC * b, NC * (b + 1)):
                            nc.scalar.activation(s[:, i], s[:, i], ACT.Identity, bias=nmr[:, i:i + 1],
                                                 scale=rstd[:, i:i + 1]).then_inc(y_ready, 1)

                    coming("t0", "t1", "t2", "t3", "l0")
                    exps(0)
                    exps(1)
                    coming("l1", "l2", "l3", "g0")
                    kt_high(0)
                    coming("g1")
                    kt_high(1)
                    coming("g2", "g3")
                    normalise(0)
                    coming("v0", "v1")
                    normalise(1)
                    coming("v2", "v3")

                with act.Fori(0, PAIRS - 1) as pair:
                    turn_of(layer * PAIRS + pair, FULL)
                turn_of(layer * PAIRS + PAIRS - 1, SHORT)

        @block.vector
        def _(dve):
            steps = [0]

            def step(ins):
                steps[0] += 1
                ins.then_inc(const_step, 1)
                dve.wait_ge(const_step, steps[0])

            dve.wait_ge(consts_loaded, 48)
            for c in range(NC):
                block_ = adj_off[:, c, c * P:(c + 1) * P]
                step(nc.vector.tensor_tensor(diag[:, 0, c], block_, ident[:], ALU.mult))
                step(nc.vector.tensor_tensor(block_, block_, diag[:, 0, c], ALU.subtract))

            def low(order, name):
                buf, i = {"t": xT2, "l": z2[0], "g": z2[1], "v": v2}[name[0]], int(name[1])
                dve.wait_ge(hi_ready, order.splits(name))
                nc.vector.tensor_tensor(buf[:, LO, i], ring[:, order.bank(name)], buf[:, HI, i].bitcast(F32),
                                        ALU.subtract).then_inc(lo_ready, 1)

            for t in range(ND):
                low(Order(FULL, 0, 0), f"t{t}")
            with dve.Fori(0, LAYERS) as layer:
                def scalar(ins, n):
                    ins.then_inc(scalar_step, 1)
                    dve.wait_ge(scalar_step, 6 * layer + n)

                scalar(nc.vector.tensor_copy(small[:, 0:1], gate_in[:, bass.ds(layer, 1)]), 1)
                scalar(nc.vector.tensor_copy(small[:, 1:2], sigma_in[:, bass.ds(layer, 1)]), 2)
                dve.wait_ge(scalar_exp, 2 * layer + 1)
                scalar(nc.vector.tensor_scalar(small[:, 3:4], small[:, 2:3], 1.0, None, ALU.add), 3)
                scalar(nc.vector.reciprocal(w_l[:], small[:, 3:4]), 4)
                scalar(nc.vector.tensor_scalar(small[:, 4:5], w_l[:], -1.0, 1.0, ALU.mult, ALU.add), 5)
                dve.wait_ge(expo_ready, 1)
                scalar(nc.vector.tensor_scalar(coef[:, BC:2 * BC], expo[:, 0:BC], 0.0, small[:, 4:5],
                                               ALU.mult, ALU.add), 6)
                dve.wait_ge(scalar_exp, 2 * layer + 2)
                nc.vector.tensor_copy(small[:, 5:6], inv_s2[:]).then_inc(coef_ready, 1)
                for i, stage in enumerate((stage_a, stage_b)):
                    dve.wait_ge(w_hi, 3 * layer + 1 + i)
                    nc.vector.tensor_tensor(wz2[i][:, LO], stage[:], wz2[i][:, HI].bitcast(F32),
                                            ALU.subtract).then_inc(w_lo, 1)
                first = opening(layer)
                for name in FIRST[:2 * ND]:
                    low(first, name)
                dve.wait_ge(w_hi, 3 * layer + 3)
                nc.vector.tensor_tensor(wvo2[:, LO], gram[:].rearrange("p g b c f -> p (g b) (c f)"),
                                        wvo2[:, HI].bitcast(F32), ALU.subtract).then_inc(w_lo, 1)
                for name in FIRST[2 * ND:]:
                    low(first, name)

                def turn_of(u, names):
                    order = turn(u, names)

                    def coming(*wanted):
                        for name in wanted:
                            if name in names:
                                low(order, name)

                    def diagonals(g, b):
                        dve.wait_ge(gram_full, 2 * B * u + B * g + b + 1)
                        for c in range(NC):
                            i = NC * b + c
                            nc.vector.tensor_tensor_reduce(
                                out=diag[:, g, i], in0=gram[:, g, b, c, c * P:(c + 1) * P], in1=ident[:],
                                scale=(1.0, -0.5)[g], scalar=0.0, op0=ALU.mult, op1=ALU.add,
                                accum_out=sq[:, g, i:i + 1]).then_inc(diag_ready, 1)

                    def gaussian_bias(b):
                        of = slice(NC * b, NC * (b + 1))
                        dve.wait_ge(diag_ready, 2 * BC * u + BC + NC * (b + 1))
                        nc.vector.tensor_scalar(gbias[:, of], sq[:, 1, of], inv_s2[:], None,
                                                ALU.mult).then_inc(gbias_ready, 1)

                    def coefs(ins, n):
                        ins.then_inc(coef_step, 1)
                        dve.wait_ge(coef_step, 5 * u + n)

                    def split_diag(g, of, nth, ready, count):
                        dve.wait_ge(ready, count)
                        nc.vector.tensor_copy(diag2[:, g, HI, of], diag[:, g, of]).then_inc(dhi_ready, 1)
                        dve.wait_ge(dhi_ready, (B + 1) * u + nth)
                        nc.vector.tensor_tensor(diag2[:, g, LO, of], diag[:, g, of],
                                                diag2[:, g, HI, of].bitcast(F32), ALU.subtract).then_inc(dlo_ready, 1)

                    def cosines(b):
                        dve.wait_ge(r_full, u + 1)
                        for c in range(NC):
                            nc.vector.tensor_tensor(adj_r[:, b, c], rbank[:, b], adj_off[:, c],
                                                    ALU.mult).then_inc(adjr_ready, 1)
                        for c in range(NC):
                            i = NC * b + c
                            dve.wait_ge(adjr_ready, BC * u + i + 1)
                            nc.vector.scalar_tensor_tensor(
                                out=t_l[:, i], in0=gram[:, 0, b, c], scalar=0.0, in1=adj_r[:, b, c],
                                op0=ALU.max, op1=ALU.mult, accum_out=deg[:, i:i + 1]).then_inc(tl_ready, 1)

                    def gaussians(b):
                        for c in range(NC):
                            i = NC * b + c
                            dve.wait_ge(eg_ready, BC * u + i + 1)
                            nc.vector.scalar_tensor_tensor(
                                out=t_g[:, i], in0=e_g[:, i], scalar=1.0, in1=adj_off[:, c],
                                op0=ALU.min, op1=ALU.mult, accum_out=deg[:, BC + i:BC + i + 1]).then_inc(tg_ready, 1)

                    def combine(b):
                        for i in range(NC * b, NC * (b + 1)):
                            nc.vector.tensor_scalar(t_g[:, i], t_g[:, i], cnorm[:, BC + i:BC + i + 1], None,
                                                    ALU.mult).then_inc(scaled, 1)
                        for i in range(NC * b, NC * (b + 1)):
                            dve.wait_ge(scaled, BC * u + i + 1)
                            nc.vector.scalar_tensor_tensor(out=km[:, i], in0=t_l[:, i], scalar=cnorm[:, i:i + 1],
                                                           in1=t_g[:, i], op0=ALU.mult, op1=ALU.add).then_inc(k_ready, 1)

                    def kt_low(b):
                        dve.wait_ge(kt_hi, B * u + b + 1)
                        nc.vector.tensor_tensor(kT2[:, LO, b], tbank[:], kT2[:, HI, b].bitcast(F32),
                                                ALU.subtract).then_inc(kt_lo, 1)

                    def residual(i):
                        dve.wait_ge(ring_full, order.fill(f"k{i}"))
                        if i == 0:
                            dve.wait_ge(xres_loaded, 16 * u + 16)
                        if i % NC == 0:
                            dve.wait_ge(y_stored, 16 * B * u)
                        nc.vector.tensor_tensor(s[:, i], ring[:, order.bank(f"k{i}")], x_res[:, i],
                                                ALU.add).then_inc(s_ready, 1)

                    def row_stats(i):
                        dve.wait_ge(s_ready, BC * u + i + 1)
                        nc.vector.bn_stats(stats[:, i], s[:, i]).then_inc(stats_ready, 1)

                    def row_moments(b):
                        of = slice(NC * b, NC * (b + 1))
                        dve.wait_ge(stats_ready, BC * u + NC * (b + 1))
                        nc.vector.memset(spare[:], 0.0)
                        for i in range(NC * b, NC * (b + 1)):
                            nc.vector.bn_aggr(mv[:, i], stats[:, i]).then_inc(mv_ready, 1)
                        dve.wait_ge(mv_ready, BC * u + NC * (b + 1))
                        nc.vector.tensor_scalar(ve[:, of], mv[:, of, 1], LN_EPS, None, ALU.add).then_inc(ve_ready, 1)
                        nc.vector.tensor_scalar(nmean[:, of], mv[:, of, 0], -1.0, None, ALU.mult).then_inc(ve_ready, 1)

                    diagonals(0, 0)
                    coming("t0")
                    diagonals(0, 1)
                    dve.wait_ge(diag_ready, 2 * BC * u + BC)
                    nc.vector.tensor_scalar(sqm[:], sq[:, 0], DEG_EPS * DEG_EPS, None, ALU.max).then_inc(sqm_ready, 1)
                    coming("t1", "t2")
                    diagonals(1, 0)
                    gaussian_bias(0)
                    coming("t3")
                    split_diag(1, slice(0, NC), 1, diag_ready, 2 * BC * u + BC + NC)
                    dve.wait_ge(rn_ready, u + 1)
                    for i in range(BC):
                        nc.vector.tensor_scalar(diag[:, 0, i], ident[:], rn[:, i:i + 1], None,
                                                ALU.mult).then_inc(dl_ready, 1)
                    split_diag(0, slice(0, BC), 2, dl_ready, BC * u + BC)
                    coefs(nc.vector.tensor_scalar(coef[:, 0:BC], rn[:], w_l[:], None, ALU.mult), 1)
                    diagonals(1, 1)
                    gaussian_bias(1)
                    split_diag(1, slice(NC, BC), 3, diag_ready, 2 * BC * u + 2 * BC)
                    coming("l0")
                    cosines(0)
                    coming("l1")
                    cosines(1)
                    gaussians(0)
                    coming("l2")
                    gaussians(1)
                    dve.wait_ge(tl_ready, BC * u + BC)
                    coefs(nc.vector.tensor_tensor(deg[:, 0:BC], deg[:, 0:BC], rn[:], ALU.mult), 2)
                    dve.wait_ge(tg_ready, BC * u + BC)
                    coefs(nc.vector.tensor_scalar(dm[:], deg[:], DEG_EPS, None, ALU.max), 3)
                    coefs(nc.vector.reciprocal(drec[:], dm[:]), 4)
                    coefs(nc.vector.tensor_tensor(cnorm[:], drec[:], coef[:], ALU.mult), 5)
                    combine(0)
                    coming("l3")
                    combine(1)
                    coming("g0")
                    kt_low(0)
                    coming("g1")
                    residual(0)
                    row_stats(0)
                    kt_low(1)
                    residual(1)
                    row_stats(1)
                    coming("g2")
                    row_moments(0)
                    residual(2)
                    row_stats(2)
                    coming("g3")
                    residual(3)
                    row_stats(3)
                    row_moments(1)
                    coming("v0", "v1", "v2", "v3")

                with dve.Fori(0, PAIRS - 1) as pair:
                    turn_of(layer * PAIRS + pair, FULL)
                turn_of(layer * PAIRS + PAIRS - 1, SHORT)

        @block.tensor
        def _(pe):
            def product(bank, lhs, rhs, ks, sem, start=True):
                n = 0
                for k in ks:
                    for l, r in PASSES:
                        ins = nc.tensor.matmul(bank, lhs(l, k), rhs(r, k), start=(start and n == 0),
                                               stop=(n == 3 * len(ks) - 1), skip_group_check=not start)
                        n += 1
                ins.then_inc(sem, 1)

            def transpose_x(t, bank):
                for i in range(BC):
                    ins = nc.tensor.transpose(ring[:, bank, i * P:(i + 1) * P], x_tr[:, i, t * P:(t + 1) * P], ident[:])
                ins.then_inc(ring_full, 1)

            def weighted(w, names, before):
                for name in names:
                    bank, i = before(name), int(name[1])
                    if name[0] == "v":
                        product(bank, lambda h, k: xT2[:, h, k, i * P:(i + 1) * P],
                                lambda h, k: w[:, h, k], range(ND), ring_full)
                    else:
                        product(bank, lambda h, k: w[:, h, k, i * P:(i + 1) * P],
                                lambda h, k: xT2[:, h, k], range(ND), ring_full)

            pe.wait_ge(xtr_loaded, 16)
            for t in range(ND):
                if t >= 2:
                    pe.wait_ge(lo_ready, t - 1)
                transpose_x(t, t % 2)
            with pe.Fori(0, LAYERS) as layer:
                first = opening(layer)

                def opened(name):
                    n = FIRST.index(name)
                    if n >= 2:
                        pe.wait_ge(lo_ready, first.splits(FIRST[n - 2]))
                    return ring[:, first.bank(name)]

                pe.wait_ge(lo_ready, first.split)
                pe.wait_ge(s_ready, BC * PAIRS * layer)
                pe.wait_ge(w_lo, 3 * layer + 1)
                weighted(wz2[0], FIRST[0:ND], opened)
                pe.wait_ge(w_lo, 3 * layer + 2)
                weighted(wz2[1], FIRST[ND:2 * ND], opened)
                pe.wait_ge(vo_loaded, 32 * layer + 32)
                for d in range(ND):
                    for f in range(ND):
                        ins = nc.tensor.matmul(gram[:, d // B, d % B].rearrange("p c f -> p (c f)"),
                                               stage_a[:, f, d * P:(d + 1) * P], stage_b[:, f],
                                               start=(f == 0), stop=(f == ND - 1))
                ins.then_inc(wvo_full, 1)
                pe.wait_ge(w_lo, 3 * layer + 3)
                weighted(wvo2, FIRST[2 * ND:], opened)

                def turn_of(u, names):
                    order = turn(u, names)

                    def free(name):
                        n = names.index(name)
                        if n < 2:
                            pe.wait_ge(lo_ready, order.split + n - 1)
                        elif names[n - 2][0] == "k":
                            pe.wait_ge(s_ready, BC * u + int(names[n - 2][1]) + 1)
                        else:
                            pe.wait_ge(lo_ready, order.splits(names[n - 2]))
                        return ring[:, order.bank(name)]

                    def coming(w, *wanted):
                        weighted(w, [name for name in wanted if name in names], free)

                    def grams(g, b):
                        if b == 0:
                            pe.wait_ge(lo_ready, order.split - (2 - g) * ND)
                        n = 0
                        for c in range(NC):
                            rows = slice(b * C + c * P, b * C + (c + 1) * P)
                            for k in range(ND):
                                for l, r in PASSES:
                                    ins = nc.tensor.matmul(
                                        gram[:, g, b, c], z2[g][:, l, k, rows], z2[g][:, r, k, b * C:(b + 1) * C],
                                        start=(n == 0), stop=(n == 2 * 3 * ND - 1), skip_group_check=True)
                                    n += 1
                        ins.then_inc(gram_full, 1)

                    def x_chunk(t):
                        if t == 0:
                            pe.wait_ge(xtr_loaded, 16 * u + 32)
                        free(f"t{t}")
                        transpose_x(t, order.bank(f"t{t}"))

                    def column_norms():
                        pe.wait_ge(dlo_ready, (B + 1) * u + 2)
                        for h in (HI, LO):
                            ins = nc.tensor.matmul(rbank[:].rearrange("p b f -> p (b f)"), ones_r[:],
                                                   diag2[:, 0, h].rearrange("p i f -> p (i f)"),
                                                   start=(h == HI), stop=(h == LO))
                        ins.then_inc(r_full, 1)

                    def add_squares(b):
                        pe.wait_ge(dlo_ready, (B + 1) * u + (1, 3)[b])
                        for c in range(NC):
                            for h in (HI, LO):
                                ins = nc.tensor.matmul(
                                    gram[:, 1, b, c], ones_r[:],
                                    diag2[:, 1, h, NC * b:NC * (b + 1)].rearrange("p i f -> p (i f)"),
                                    start=False, stop=(c == NC - 1 and h == LO), skip_group_check=True)
                        ins.then_inc(sq_added, 1)

                    def transposed_k(b):
                        pe.wait_ge(k_ready, BC * u + NC * (b + 1))
                        pe.wait_ge(kt_lo, B * u + b)
                        for m in range(NC):
                            for c in range(NC):
                                ins = nc.tensor.transpose(tbank[:, m, c * P:(c + 1) * P],
                                                          km[:, NC * b + c, m * P:(m + 1) * P], ident[:])
                        ins.then_inc(kt_full, 1)

                    def kv(i):
                        b, c = i // NC, i % NC
                        pe.wait_ge(kt_lo, B * u + b + 1)
                        product(free(f"k{i}"), lambda h, m: kT2[:, h, b, m, c * P:(c + 1) * P],
                                lambda h, m: v2[:, h, NC * b + m], range(NC), ring_full)

                    grams(0, 0)
                    x_chunk(0)
                    grams(0, 1)
                    x_chunk(1)
                    x_chunk(2)
                    grams(1, 0)
                    x_chunk(3)
                    grams(1, 1)
                    if "l0" in names:
                        pe.wait_ge(lo_ready, order.splits("t3"))
                    coming(wz2[0], "l0")
                    column_norms()
                    add_squares(0)
                    add_squares(1)
                    coming(wz2[0], "l1", "l2", "l3")
                    coming(wz2[1], "g0")
                    transposed_k(0)
                    coming(wz2[1], "g1")
                    kv(0)
                    transposed_k(1)
                    kv(1)
                    coming(wz2[1], "g2")
                    kv(2)
                    coming(wz2[1], "g3")
                    kv(3)
                    coming(wvo2, "v0", "v1", "v2", "v3")

                with pe.Fori(0, PAIRS - 1) as pair:
                    turn_of(layer * PAIRS + pair, FULL)
                turn_of(layer * PAIRS + PAIRS - 1, SHORT)


def build(nc, x, adj, adjT, columns, bm, bias, wlT, wgT, wv, woT, gate, log_sigma, out):
    with ExitStack() as ctx:
        ident = ctx.enter_context(nc.sbuf_tensor("ident", [P, P], F32))
        ones = ctx.enter_context(nc.sbuf_tensor("ones", [P, P], F32))
        ones_r = ctx.enter_context(nc.sbuf_tensor("ones_r", [P, P], F32R))
        ident_zero = ctx.enter_context(nc.semaphore("ident_zero"))
        ones_done = ctx.enter_context(nc.semaphore("ones_done"))
        with nc.Block() as block:
            @block.gpsimd
            def _(pool):
                nc.gpsimd.memset(ident[:], 0.0).then_inc(ident_zero, 1)
                pool.wait_ge(ident_zero, 1)
                nc.gpsimd.affine_select(out=ident[:], in_=ident[:], compare_op=ALU.not_equal, fill=1.0, base=0,
                                        pattern=[[-1, P]], channel_multiplier=1)

            @block.vector
            def _(dve):
                nc.vector.memset(ones[:], 1.0).then_inc(ones_done, 1)
                dve.wait_ge(ones_done, 1)
                nc.vector.tensor_copy(ones_r[:], ones[:])

        setup = {"ident": ident, "ones": ones, "ones_r": ones_r}
        attention_and_hop(nc, setup, x, adj, adjT, columns, bm, bias, out)
        kernel_similarity_layers(nc, setup, adj, wlT, wgT, wv, woT, gate, log_sigma, out)


def kernel(**inputs):
    import numpy as np
    import concourse.bacc as bacc
    from concourse.bass_utils import run_bass_kernel_spmd as run

    def layers(name, turn):
        both = [np.asarray(inputs[f"L{i}_gnn_{name}"]) for i in (2, 3)]
        return np.ascontiguousarray(np.stack([w.T if turn else w for w in both]))

    def columns(*names):
        return np.ascontiguousarray(np.stack([np.asarray(inputs[n]).reshape(-1, P).T for n in names], axis=1))

    arrays = {
        "x": np.asarray(inputs["x"]),
        "adj": np.asarray(inputs["adj"]),
        "adjT": np.ascontiguousarray(np.asarray(inputs["adj"]).T),
        "columns": columns("L0_gnn_wq", "L0_gnn_wk"),
        "bm": np.asarray(inputs["L0_gnn_bm"]),
        "bias": np.asarray(inputs["L1_gnn_bias"]),
        "wlT": layers("W_lang", True),
        "wgT": layers("W_grav", True),
        "wv": layers("W_V", False),
        "woT": layers("W_O", True),
        "gate": layers("gate_logit", False),
        "log_sigma": layers("log_sigma", False),
    }
    nc = bacc.Bacc("TRN2", target_bir_lowering=False, num_devices=1)
    args = [nc.dram_tensor(f"in_{k}", a.shape, mybir.dt.from_np(a.dtype), kind="ExternalInput").ap()
            for k, a in arrays.items()]
    out = nc.dram_tensor("out_x", arrays["x"].shape, F32, kind="ExternalOutput").ap()
    build(nc, *args, out)
    r = run(nc, [{f"in_{k}": a for k, a in arrays.items()}], core_ids=[0])
    return r.results[0]["out_x"]
```

```python
from contextlib import ExitStack

import concourse.bass as bass
from concourse import mybir

F32 = mybir.dt.float32
F32R = mybir.dt.float32r
ALU = mybir.AluOpType
ACT = mybir.ActivationFunctionType
AX = mybir.AxisListType

P = 128
LN_EPS = 1e-5
DEG_EPS = 1e-8
SLOPE = 0.01

HI, LO = 0, 1
PASSES = ((HI, HI), (LO, HI), (HI, LO))


def weight_chunks(w):
    return w.rearrange("(k p) e -> p k e", p=P)


def pair_chunks(out, pair, b):
    return out.rearrange("(g b) (c p) f -> g p (b c) f", b=b, p=P)[pair]


class LayerOperands:

    BATCHES = 2

    def __init__(self, nc, ctx, out, adj, wlT, wgT, wv, woT, gate, log_sigma):
        self.wv, self.woT = wv, woT
        self.nc, self.out, self.adj = nc, out, adj
        self.wlT, self.wgT, self.gate, self.log_sigma = wlT, wgT, gate, log_sigma
        _, C, D = out.shape

        def sb(name, shape, dt=F32):
            return ctx.enter_context(nc.sbuf_tensor("l_" + name, shape, dt))

        self.wz2 = [sb("wl2", [P, 2, D // P, D], F32R), sb("wg2", [P, 2, D // P, D], F32R)]
        self.stage_a = sb("stage_a", [P, D // P, D])
        self.stage_b = sb("stage_b", [P, D // P, D])
        self.adj_off = sb("adj_off", [P, C // P, C])
        self.gate_in = sb("gate_in", [P, gate.shape[0]])
        self.sigma_in = sb("sigma_in", [P, gate.shape[0]])
        self.x_tr = sb("x_tr", [P, self.BATCHES * C // P, D])
        self.consts_loaded = ctx.enter_context(nc.semaphore("l_consts_loaded"))
        self.xtr_loaded = ctx.enter_context(nc.semaphore("l_xtr_loaded"))
        self.z_loaded = ctx.enter_context(nc.semaphore("l_z_loaded"))
        self.wide = ctx.enter_context(nc.psum_tensor("wide", [P, D // P, D], F32))
        self.vo_loaded = ctx.enter_context(nc.semaphore("l_vo_loaded"))
        self.wvo_full = ctx.enter_context(nc.semaphore("l_wvo_full"))
        self.w_hi = ctx.enter_context(nc.semaphore("l_w_hi"))
        self.w_lo = ctx.enter_context(nc.semaphore("l_w_lo"))

    def load_first_vo(self, sp, stages):
        for w, parts in zip((self.wv, self.woT), stages):
            at = 0
            for tile, chunks in parts:
                sp.dma_start(tile, weight_chunks(w[0])[:, at:at + chunks]).then_inc(self.vo_loaded, 16)
                at += chunks
        self.first_vo_loads = sum(len(parts) for parts in stages)

    def load_vo(self, sp, layer):
        sp.dma_start(self.stage_a[:], weight_chunks(self.wv[layer])).then_inc(self.vo_loaded, 16)
        sp.dma_start(self.stage_b[:], weight_chunks(self.woT[layer])).then_inc(self.vo_loaded, 16)

    def vo_product(self, pe, layer, stage_v, stage_o, chunks):
        pe.wait_ge(self.vo_loaded, 32 * layer + 16 * self.first_vo_loads)
        last = self.wide.shape[1] - 1
        for d in chunks:
            for f in range(last + 1):
                ins = self.nc.tensor.matmul(self.wide[:, d], stage_v[f][:, d * P:(d + 1) * P], stage_o[f],
                                            start=(f == 0), stop=(f == last))
        if d == last:
            ins.then_inc(self.wvo_full, 1)

    def weight_high(self, act, layer, i):
        act.wait_ge(self.z_loaded, 32 * layer + 32)
        self.nc.scalar.activation(self.wz2[i][:, HI], (self.stage_a, self.stage_b)[i][:],
                                  ACT.Copy).then_inc(self.w_hi, 1)

    def weight_low(self, dve, layer, i):
        dve.wait_ge(self.w_hi, 3 * layer + 1 + i)
        self.nc.vector.tensor_tensor(self.wz2[i][:, LO], (self.stage_a, self.stage_b)[i][:],
                                     self.wz2[i][:, HI].bitcast(F32), ALU.subtract).then_inc(self.w_lo, 1)

    def load(self, sp, first):
        if first:
            sp.dma_start(self.x_tr[:], pair_chunks(self.out, 0, self.BATCHES)).then_inc(self.xtr_loaded, 16)
            sp.dma_start(self.stage_a[:], weight_chunks(self.wlT[0])).then_inc(self.z_loaded, 16)
        else:
            sp.dma_start(self.stage_b[:], weight_chunks(self.wgT[0])).then_inc(self.z_loaded, 16)
            sp.dma_start(self.adj_off[:],
                         self.adj.rearrange("(c p) f -> p c f", p=P)).then_inc(self.consts_loaded, 16)
            sp.dma_start(self.gate_in[:], self.gate.partition_broadcast(P)).then_inc(self.consts_loaded, 16)
            sp.dma_start(self.sigma_in[:], self.log_sigma.partition_broadcast(P)).then_inc(self.consts_loaded, 16)


def attention_and_hop(nc, setup, x, adj, adjT, columns, bm, bias, out, coming):
    BATCH, C, N = x.shape
    NC, NN = C // P, N // P
    YW = C + 2
    LO_ROW = 32
    ident, ones, ones_r = setup["ident"], setup["ones"], setup["ones_r"]

    with ExitStack() as ctx:
        def sb(name, shape, dt=F32):
            return ctx.enter_context(nc.sbuf_tensor("a_" + name, shape, dt))

        def ps(name, shape):
            return ctx.enter_context(nc.psum_tensor("a_" + name, shape, F32))

        def sem(name):
            return ctx.enter_context(nc.semaphore("a_" + name))

        adjq = sb("adjq", [P, NC, YW])
        adjq2 = sb("adjq2", [P, 2, NC, YW], F32R)
        adjn = sb("adjn", [P, NC, C])
        hop = sb("hop", [P, NC, C])
        hop2 = sb("hop2", [P, 2, NC, C], F32R)
        cols = sb("cols", [P, 2, NC])
        wkb = sb("wkb", [P, NC, P])
        wkb2 = sb("wkb2", [P, 2, NC, P], F32R)
        bmb = sb("bmb", [P, C])
        biasb = sb("biasb", [LO_ROW + 1, N])
        bias_hi = sb("bias_hi", [LO_ROW + 1, N], F32R)
        bias2 = sb("bias2", [LO_ROW + 1, N], F32R)
        nhalf = sb("nhalf", [P, NC])
        spare = sb("spare", [P, 1])

        x_in = sb("x_in", [P, NC, N])
        x2 = sb("x2", [P, 2, NC, N], F32R)
        x_res = sb("x_res", [P, NC, N])
        more_stage = sb("more_stage", [P, 2, N])
        y2 = [sb(f"y2_{i}", [P, 2, NN, YW], F32R) for i in range(2)]
        e2 = [sb(f"e2_{i}", [P, 2, NN, N], F32R) for i in range(2)]
        qcol = sb("qcol", [P, NN])
        qtop = sb("qtop", [P, 1])
        qdiag = sb("qdiag", [P, P])
        qmax = sb("qmax", [P, 1])
        qs = sb("qs", [P, NN])
        ea = sb("ea", [P, NN])
        eb = sb("eb", [P, NN])
        karg = sb("karg", [P, 2, N])
        kexp = sb("kexp", [P, 2, N])
        e1 = sb("e1", [P, 2, N])
        e = sb("e", [P, NN, N])
        rden = sb("rden", [P, NN])
        oT = sb("oT", [P, NN, C])
        s0 = sb("s0", [P, NC, N])
        stats = sb("stats", [P, 2, NC, 6])
        mv = sb("mv", [P, 2, NC, 2])
        ve = sb("ve", [P, 2, NC])
        rstd = sb("rstd", [P, 2, NC])
        nmean = sb("nmean", [P, 2, NC])
        nmr = sb("nmr", [P, 2, NC])
        x1 = sb("x1", [P, NC, N])
        x12 = sb("x12", [P, 2, NC, N], F32R)
        s1 = [sb(f"s1_{i}", [P, NC, N]) for i in range(2)]
        yout = sb("yout", [P, NC, N])

        BANK = 512
        agg = coming.wide
        stage_vo = (((x_in[:], 2), (karg[:], 2)),
                    ((more_stage[:], 2), (adjn[:].rearrange("p c f -> p (c f)").unsqueeze(1), 1),
                     (hop[:].rearrange("p c f -> p (c f)").unsqueeze(1), 1)))
        stage_v, stage_o = ([tile[:, i] for tile, chunks in parts for i in range(chunks)] for parts in stage_vo)
        kbank = ps("kbank", [P, N])
        ring = ps("ring", [P, 2, BANK])
        qbank = ps("qbank", [P, P])

        const_loaded = sem("const_loaded")
        const_step = sem("const_step")
        adjq_ready = sem("adjq_ready")
        wk_ready = sem("wk_ready")
        hop_ready = sem("hop_ready")
        nhalf_ready = sem("nhalf_ready")
        ones_ready = sem("ones_ready")
        bias_ready = sem("bias_ready")
        x_loaded = sem("x_loaded")
        xres_loaded = sem("xres_loaded")
        x_hi = sem("x_hi")
        x_lo = sem("x_lo")
        y_full = sem("y_full")
        y_hi = sem("y_hi")
        y_lo = sem("y_lo")
        q_copied = sem("q_copied")
        q_step = sem("q_step")
        k_full = sem("k_full")
        q_full = sem("q_full")
        karg_ready = sem("karg_ready")
        kexp_ready = sem("kexp_ready")
        qexp_ready = sem("qexp_ready")
        e1_ready = sem("e1_ready")
        e_ready = sem("e_ready")
        e_hi = sem("e_hi")
        e_lo = sem("e_lo")
        agg_full = sem("agg_full")
        rden_ready = sem("rden_ready")
        oT_ready = sem("oT_ready")
        o_full = sem("o_full")
        s0_ready = sem("s0_ready")
        s0_stats = sem("s0_stats")
        hop_stats = sem("hop_stats")
        mv_ready = [sem(f"mv_ready_{i}") for i in (0, 1)]
        ve_ready = [sem(f"ve_ready_{i}") for i in (0, 1)]
        ln_step = [sem(f"ln_step_{i}") for i in (0, 1)]
        x1_ready = sem("x1_ready")
        x1_hi = sem("x1_hi")
        x1_lo_pool = sem("x1_lo_pool")
        x1_lo_dve = sem("x1_lo_dve")
        hop_full = sem("hop_full")
        s1_ready = sem("s1_ready")
        y_ready = sem("y_ready")
        y_stored = sem("y_stored")

        def nodes(ap):
            return ap.rearrange("(c p) f -> p c f", p=P)

        def turns(engine, turn):
            for n in range(4):
                turn(n, n % 2, n >= 1, n >= 2, n >= 3, True, True)
            with engine.Fori(2, BATCH // 2 - 1) as half:
                turn(2 * half, 0, True, True, True, True, True)
                turn(2 * half + 1, 1, True, True, True, True, True)
            turn(BATCH - 2, 0, True, True, True, True, False)
            turn(BATCH - 1, 1, True, True, True, False, False)

        block = ctx.enter_context(nc.Block())

        @block.sync
        def _(sp):
            def load_x(m):
                sp.dma_start(x_in[:], nodes(x[m])).then_inc(x_loaded, 16)

            def load_residual(n):
                sp.wait_ge(s0_ready, NC * n)
                sp.dma_start(x_res[:], nodes(x[n])).then_inc(xres_loaded, 16)

            def store(n):
                sp.wait_ge(y_ready, NC * n + NC)
                sp.dma_start(nodes(out[n]), yout[:]).then_inc(y_stored, 16)

            load_x(0)
            sp.dma_start(adjq[:, :, 0:C], nodes(adjT)).then_inc(const_loaded, 16)
            sp.dma_start(cols[:], columns).then_inc(const_loaded, 16)
            sp.dma_start(adjn[:], nodes(adj)).then_inc(const_loaded, 16)
            sp.dma_start(bmb[:], bm.partition_broadcast(P)).then_inc(const_loaded, 16)
            sp.dma_start(biasb[:], bias.partition_broadcast(LO_ROW + 1)).then_inc(const_loaded, 16)
            for m in (1, 2):
                sp.wait_ge(x_lo, m)
                load_x(m)
            for n in range(3):
                load_residual(n)
                sp.wait_ge(x_lo, n + 3)
                load_x(n + 3)
            with sp.Fori(3, BATCH - 3) as n:
                load_residual(n)
                store(n - 3)
                sp.wait_ge(x_lo, n + 3)
                load_x(n + 3)
            sp.wait_ge(y_stored, 16 * coming.BATCHES)
            for n in range(BATCH - 3, BATCH - 1):
                load_residual(n)
                store(n - 3)
                coming.load(sp, n == BATCH - 3)
            sp.wait_ge(hop_ready, 1)
            sp.wait_ge(x_lo, BATCH)
            sp.wait_ge(kexp_ready, 2 * BATCH)
            coming.load_first_vo(sp, stage_vo)
            load_residual(BATCH - 1)
            store(BATCH - 4)
            for n in range(BATCH - 3, BATCH):
                store(n)
            sp.wait_ge(y_stored, 16 * BATCH)

        @block.gpsimd
        def _(pool):
            nc.gpsimd.memset(nhalf[:], -0.5).then_inc(nhalf_ready, 1)
            pool.wait_ge(nhalf_ready, 1)
            for i in range(2):
                nc.gpsimd.memset(y2[i][:, HI, :, C:YW].bitcast(F32), 1.0).then_inc(ones_ready, 1)
                nc.gpsimd.memset(y2[i][:, LO, :, C:YW].bitcast(F32), 0.0).then_inc(ones_ready, 1)

            def split_x(m):
                pool.wait_ge(x_hi, m + 1)
                nc.gpsimd.tensor_tensor(x2[:, LO], x_in[:], x2[:, HI].bitcast(F32), ALU.subtract).then_inc(x_lo, 1)

            def e_low(m, par, c):
                pool.wait_ge(e_hi, NN * m + c + 1)
                nc.gpsimd.tensor_tensor(e2[par][:, LO, c], e[:, c], e2[par][:, HI, c].bitcast(F32),
                                        ALU.subtract).then_inc(e_lo, 1)

            def norm_scalars(which, m):
                pool.wait_ge(ve_ready[which], 2 * m + 2)
                if which == 1:
                    pool.wait_ge(y_ready, NC * m)
                nc.gpsimd.tensor_tensor(rstd[:, which], ve[:, which], nhalf[:], ALU.pow).then_inc(ln_step[which], 1)
                pool.wait_ge(ln_step[which], 2 * m + 1)
                nc.gpsimd.tensor_tensor(nmr[:, which], nmean[:, which], rstd[:, which],
                                        ALU.mult).then_inc(ln_step[which], 1)

            def x1_low(m):
                pool.wait_ge(x1_ready, NC * m + 1)
                pool.wait_ge(x1_hi, NC * m + 1)
                nc.gpsimd.tensor_tensor(x12[:, LO, 0], x1[:, 0], x12[:, HI, 0].bitcast(F32),
                                        ALU.subtract).then_inc(x1_lo_pool, 1)

            def turn(n, par, before, earlier, earliest, coming, later):
                e_low(n, par, 2)
                if before:
                    norm_scalars(0, n - 1)
                e_low(n, par, 3)
                if before:
                    x1_low(n - 1)
                if later:
                    split_x(n + 2)
                if coming:
                    e_low(n + 1, 1 - par, 0)
                    e_low(n + 1, 1 - par, 1)
                if earlier:
                    norm_scalars(1, n - 2)

            split_x(0)
            split_x(1)
            for c in range(NN - 2):
                e_low(0, 0, c)
            turns(pool, turn)
            norm_scalars(0, BATCH - 1)
            x1_low(BATCH - 1)
            norm_scalars(1, BATCH - 2)
            norm_scalars(1, BATCH - 1)

        @block.scalar
        def _(act):
            def x_high(m):
                act.wait_ge(x_loaded, 16 * m + 16)
                act.wait_ge(y_full, NN * m)
                nc.scalar.activation(x2[:, HI], x_in[:], ACT.Copy).then_inc(x_hi, 1)

            def y_high(m, par, c):
                act.wait_ge(y_full, NN * m + c + 1)
                nc.scalar.activation(y2[par][:, HI, c, 0:C], ring[:, c % 2, 0:C], ACT.Copy).then_inc(y_hi, 1)

            def exponentials(m):
                act.wait_ge(q_step, 5 * m + 4)
                nc.scalar.activation(ea[:], qs[:], ACT.Exp).then_inc(qexp_ready, 1)
                nc.scalar.activation(eb[:], qs[:], ACT.Exp, scale=SLOPE).then_inc(qexp_ready, 1)
                for i, scale in ((0, 1.0 - SLOPE), (1, SLOPE - 1.0)):
                    act.wait_ge(karg_ready, 2 * m + i + 1)
                    nc.scalar.activation(kexp[:, i], karg[:, i], ACT.Exp, scale=scale).then_inc(kexp_ready, 1)

            def e_first(m, c):
                if c == 0:
                    act.wait_ge(kexp_ready, 2 * m + 1)
                    act.wait_ge(qexp_ready, 2 * m + 2)
                nc.scalar.activation(e1[:, c % 2], kexp[:, 0], ACT.Copy, scale=ea[:, c:c + 1]).then_inc(e1_ready, 1)

            def e_high(m, par, c):
                act.wait_ge(e_ready, NN * m + c + 1)
                nc.scalar.activation(e2[par][:, HI, c], e[:, c], ACT.Copy).then_inc(e_hi, 1)

            def x1_high(m):
                act.wait_ge(ln_step[0], 2 * m + 2)
                act.wait_ge(hop_full, NC * m)
                for c in range(NC):
                    nc.scalar.activation(x12[:, HI, c], s0[:, c], ACT.Identity, bias=nmr[:, 0, c:c + 1],
                                         scale=rstd[:, 0, c:c + 1]).then_inc(x1_hi, 1)

            def hop_out(m, par, c):
                act.wait_ge(hop_full, NC * m + c + 1)
                nc.scalar.activation(s1[par][:, c], ring[:, c % 2], ACT.Copy).then_inc(s1_ready, 1)

            def second_norm(m, par):
                act.wait_ge(ln_step[1], 2 * m + 2)
                act.wait_ge(y_stored, 16 * m)
                for c in range(NC):
                    nc.scalar.activation(yout[:, c], s1[par][:, c], ACT.Identity, bias=nmr[:, 1, c:c + 1],
                                         scale=rstd[:, 1, c:c + 1]).then_inc(y_ready, 1)

            def turn(n, par, before, earlier, earliest, coming, later):
                if coming:
                    y_high(n + 1, 1 - par, 0)
                    y_high(n + 1, 1 - par, 1)
                e_first(n, 3)
                if coming:
                    y_high(n + 1, 1 - par, 2)
                e_high(n, par, 2)
                e_high(n, par, 3)
                if coming:
                    y_high(n + 1, 1 - par, 3)
                if earliest:
                    second_norm(n - 3, 1 - par)
                if before:
                    x1_high(n - 1)
                if later:
                    x_high(n + 2)
                if coming:
                    exponentials(n + 1)
                    e_first(n + 1, 0)
                    e_first(n + 1, 1)
                if before:
                    hop_out(n - 1, 1 - par, 0)
                if coming:
                    e_high(n + 1, 1 - par, 0)
                if before:
                    hop_out(n - 1, 1 - par, 1)
                if coming:
                    e_first(n + 1, 2)
                    e_high(n + 1, 1 - par, 1)

            x_high(0)
            for c in range(NN):
                y_high(0, 0, c)
            x_high(1)
            exponentials(0)
            e_first(0, 0)
            e_first(0, 1)
            e_high(0, 0, 0)
            e_first(0, 2)
            e_high(0, 0, 1)
            turns(act, turn)
            x1_high(BATCH - 1)
            second_norm(BATCH - 3, 1)
            for i in range(2):
                coming.weight_high(act, 0, i)
            second_norm(BATCH - 2, 0)
            for c in range(NC):
                hop_out(BATCH - 1, 1, c)
            second_norm(BATCH - 1, 1)

        @block.vector
        def _(dve):
            steps = [0]

            def step(ins):
                steps[0] += 1
                ins.then_inc(const_step, 1)
                dve.wait_ge(const_step, steps[0])

            nc.vector.memset(bias2[:].bitcast(F32), 0.0).then_inc(bias_ready, 1)
            step(nc.vector.memset(adjq[:, :, C + 1:C + 2], 0.0))
            dve.wait_ge(const_loaded, 16 * 5)
            step(nc.vector.tensor_copy(adjq[:, :, C], cols[:, 0]))
            step(nc.vector.tensor_copy(adjq2[:, HI], adjq[:]))
            nc.vector.tensor_tensor(adjq2[:, LO], adjq[:], adjq2[:, HI].bitcast(F32),
                                    ALU.subtract).then_inc(adjq_ready, 1)
            for c in range(NC):
                step(nc.vector.tensor_scalar(wkb[:, c], ones[:], cols[:, 1, c:c + 1], None, ALU.mult))
            step(nc.vector.tensor_copy(wkb2[:, HI], wkb[:]))
            nc.vector.tensor_tensor(wkb2[:, LO], wkb[:], wkb2[:, HI].bitcast(F32), ALU.subtract).then_inc(wk_ready, 1)
            step(nc.vector.tensor_tensor(hop[:], adjn[:], adjn[:], ALU.mult))
            for c in range(NC):
                step(nc.vector.tensor_tensor(hop[:, c, c * P:(c + 1) * P], hop[:, c, c * P:(c + 1) * P], ident[:],
                                             ALU.add))
            step(nc.vector.tensor_copy(hop2[:, HI], hop[:]))
            nc.vector.tensor_tensor(hop2[:, LO], hop[:], hop2[:, HI].bitcast(F32), ALU.subtract).then_inc(hop_ready, 1)
            dve.wait_ge(bias_ready, 1)
            nc.vector.tensor_copy(bias2[0:1], biasb[0:1]).then_inc(bias_ready, 1)
            step(nc.vector.tensor_copy(bias_hi[:], biasb[:]))
            nc.vector.tensor_tensor(bias2[LO_ROW:LO_ROW + 1], biasb[LO_ROW:LO_ROW + 1],
                                    bias_hi[LO_ROW:LO_ROW + 1].bitcast(F32), ALU.subtract).then_inc(bias_ready, 1)

            def y_low(m, par, c):
                dve.wait_ge(y_hi, NN * m + c + 1)
                nc.vector.tensor_copy(qcol[:, c:c + 1], ring[:, c % 2, C:C + 1]).then_inc(q_copied, 1)
                nc.vector.tensor_tensor(y2[par][:, LO, c, 0:C], ring[:, c % 2, 0:C],
                                        y2[par][:, HI, c, 0:C].bitcast(F32), ALU.subtract).then_inc(y_lo, 1)

            def q_diagonal(m):
                dve.wait_ge(q_copied, NN * m + NN)
                nc.vector.tensor_reduce(qtop[:], qcol[:], AX.X, ALU.max).then_inc(q_step, 1)
                dve.wait_ge(q_step, 5 * m + 1)
                nc.vector.tensor_scalar(qdiag[:], ident[:], qtop[:], None, ALU.mult).then_inc(q_step, 1)

            def q_shifted(m):
                dve.wait_ge(q_full, m + 1)
                nc.vector.tensor_reduce(qmax[:], qbank[:], AX.X, ALU.max).then_inc(q_step, 1)
                dve.wait_ge(q_step, 5 * m + 3)
                nc.vector.tensor_scalar(qs[:], qcol[:], qmax[:], None, ALU.subtract).then_inc(q_step, 1)

            def k_shifted(m):
                dve.wait_ge(k_full, m + 1)
                dve.wait_ge(kexp_ready, 2 * m)
                nc.vector.tensor_scalar(karg[:, 0], kbank[:], qmax[:], 0.0, ALU.add, ALU.min).then_inc(karg_ready, 1)
                nc.vector.tensor_scalar(karg[:, 1], kbank[:], qmax[:], 0.0, ALU.add, ALU.max).then_inc(karg_ready, 1)
                nc.vector.memset(spare[:], 0.0).then_inc(q_step, 1)

            def e_max(m, c):
                dve.wait_ge(e1_ready, NN * m + c + 1)
                if c == 0:
                    dve.wait_ge(kexp_ready, 2 * m + 2)
                    dve.wait_ge(e_lo, NN * m)
                nc.vector.scalar_tensor_tensor(out=e[:, c], in0=kexp[:, 1], scalar=eb[:, c:c + 1],
                                               in1=e1[:, c % 2], op0=ALU.mult, op1=ALU.max).then_inc(e_ready, 1)

            def x1_low(m):
                dve.wait_ge(x1_ready, NC * m + NC)
                dve.wait_ge(x1_hi, NC * m + NC)
                nc.vector.tensor_tensor(x12[:, LO, 1], x1[:, 1], x12[:, HI, 1].bitcast(F32),
                                        ALU.subtract).then_inc(x1_lo_dve, 1)

            def outputs(n):
                dve.wait_ge(agg_full, n + 1)
                nc.vector.reciprocal(rden[:], agg[:, :, C]).then_inc(rden_ready, 1)
                dve.wait_ge(rden_ready, n + 1)
                for i in range(NN):
                    nc.vector.scalar_tensor_tensor(out=oT[:, i], in0=agg[:, i, 0:C], scalar=rden[:, i:i + 1],
                                                   in1=bmb[:], op0=ALU.mult, op1=ALU.add).then_inc(oT_ready, 1)

            def first_residual(m, c):
                dve.wait_ge(o_full, NC * m + c + 1)
                dve.wait_ge(xres_loaded, 16 * m + 16)
                nc.vector.scalar_tensor_tensor(out=s0[:, c], in0=ring[:, c % 2], scalar=0.0, in1=x_res[:, c],
                                               op0=ALU.max, op1=ALU.add).then_inc(s0_ready, 1)

            def s0_row_stats(m, c):
                dve.wait_ge(s0_ready, NC * m + c + 1)
                nc.vector.bn_stats(stats[:, 0, c], s0[:, c]).then_inc(s0_stats, 1)

            def hop_row_stats(m, par, c):
                dve.wait_ge(s1_ready, NC * m + c + 1)
                nc.vector.bn_stats(stats[:, 1, c], s1[par][:, c]).then_inc(hop_stats, 1)

            def row_moments(which, m):
                dve.wait_ge(ln_step[which], 2 * m)
                dve.wait_ge((s0_stats, hop_stats)[which], NC * m + NC)
                nc.vector.memset(spare[:], 0.0)
                for c in range(NC):
                    nc.vector.bn_aggr(mv[:, which, c], stats[:, which, c]).then_inc(mv_ready[which], 1)
                dve.wait_ge(mv_ready[which], NC * m + NC)
                nc.vector.tensor_scalar(ve[:, which], mv[:, which, :, 1], LN_EPS, None,
                                        ALU.add).then_inc(ve_ready[which], 1)
                nc.vector.tensor_scalar(nmean[:, which], mv[:, which, :, 0], -1.0, None,
                                        ALU.mult).then_inc(ve_ready[which], 1)

            def first_norm(m):
                dve.wait_ge(ln_step[0], 2 * m + 2)
                for c in range(NC):
                    nc.vector.tensor_scalar(x1[:, c], s0[:, c], rstd[:, 0, c:c + 1], nmr[:, 0, c:c + 1],
                                            ALU.mult, ALU.add).then_inc(x1_ready, 1)

            def turn(n, par, before, earlier, earliest, coming, later):
                if earlier:
                    hop_row_stats(n - 2, par, 0)
                if before:
                    first_residual(n - 1, 0)
                e_max(n, 2)
                if before:
                    first_residual(n - 1, 1)
                    s0_row_stats(n - 1, 0)
                if coming:
                    y_low(n + 1, 1 - par, 0)
                if before:
                    s0_row_stats(n - 1, 1)
                if coming:
                    y_low(n + 1, 1 - par, 1)
                e_max(n, 3)
                if before:
                    row_moments(0, n - 1)
                if earlier:
                    hop_row_stats(n - 2, par, 1)
                if coming:
                    y_low(n + 1, 1 - par, 2)
                    y_low(n + 1, 1 - par, 3)
                    q_diagonal(n + 1)
                if earlier:
                    row_moments(1, n - 2)
                if before:
                    first_norm(n - 1)
                if coming:
                    q_shifted(n + 1)
                    k_shifted(n + 1)
                if before:
                    x1_low(n - 1)
                outputs(n)
                if coming:
                    e_max(n + 1, 0)
                    e_max(n + 1, 1)

            for c in range(NN):
                y_low(0, 0, c)
            q_diagonal(0)
            q_shifted(0)
            k_shifted(0)
            for c in range(NN - 2):
                e_max(0, c)
            turns(dve, turn)
            for c in range(NC):
                first_residual(BATCH - 1, c)
                s0_row_stats(BATCH - 1, c)
            row_moments(0, BATCH - 1)
            hop_row_stats(BATCH - 2, 0, 0)
            first_norm(BATCH - 1)
            x1_low(BATCH - 1)
            hop_row_stats(BATCH - 2, 0, 1)
            row_moments(1, BATCH - 2)
            for i in range(2):
                coming.weight_low(dve, 0, i)
            for c in range(NC):
                hop_row_stats(BATCH - 1, 1, c)
            row_moments(1, BATCH - 1)

        @block.tensor
        def _(pe):
            def y_chunks(m, before):
                for c in range(NN):
                    if c >= 2:
                        pe.wait_ge(y_lo, NN * m + c - 1)
                    elif before:
                        pe.wait_ge(s0_ready, NC * (m - 2) + c + 1)
                    else:
                        pe.wait_ge(y_lo, NN * m)
                    mm = 0
                    for l, r in PASSES:
                        for k in range(NC):
                            ins = nc.tensor.matmul(ring[:, c % 2, 0:YW], x2[:, l, k, c * P:(c + 1) * P],
                                                   adjq2[:, r, k], start=(mm == 0), stop=(mm == 3 * NC - 1))
                            mm += 1
                    ins.then_inc(y_full, 1)

            def keys(m):
                pe.wait_ge(x_lo, m + 1)
                pe.wait_ge(karg_ready, 2 * m)
                mm = 0
                for l, r in PASSES:
                    for k in range(NC):
                        ins = nc.tensor.matmul(kbank[:], wkb2[:, l, k], x2[:, r, k],
                                               start=(mm == 0), stop=(mm == 3 * NC - 1))
                        mm += 1
                ins.then_inc(k_full, 1)

            def spread_q(m):
                pe.wait_ge(q_step, 5 * m + 2)
                nc.tensor.matmul(qbank[:], ones[:], qdiag[:], start=True, stop=True).then_inc(q_full, 1)

            def attention(n, par, c):
                pe.wait_ge(e_lo, NN * n + c + 1)
                for i in range(NN):
                    for l, r in PASSES:
                        ins = nc.tensor.matmul(agg[:, i, 0:YW], e2[par][:, l, c, i * P:(i + 1) * P], y2[par][:, r, c],
                                               start=(c == 0 and (l, r) == PASSES[0]),
                                               stop=(c == NN - 1 and (l, r) == PASSES[-1]))
                if c == NN - 1:
                    ins.then_inc(agg_full, 1)

            def attention_out(m, c, earlier):
                if c == 0:
                    pe.wait_ge(oT_ready, NN * m + NN)
                if earlier:
                    pe.wait_ge(s1_ready, NC * (m - 1) + c + 1)
                else:
                    pe.wait_ge(y_lo, NN * (m + 1) + NN)
                for i in range(NN):
                    ins = nc.tensor.transpose(ring[:, c % 2, i * P:(i + 1) * P], oT[:, i, c * P:(c + 1) * P],
                                              ident[:])
                ins.then_inc(o_full, 1)

            def hops(m, coming):
                for i in range(NC):
                    if coming:
                        pe.wait_ge(y_lo, NN * (m + 2) + NN - NC + i + 1)
                    else:
                        pe.wait_ge(s0_ready, NC * m + i + 1)
                    nc.tensor.matmul(ring[:, i % 2], ones_r[0:LO_ROW + 1], bias2[:], start=True, stop=False)
                    for k in range(NC):
                        if i == 0:
                            pe.wait_ge((x1_lo_pool, x1_lo_dve)[k], m + 1)
                        for l, r in PASSES:
                            ins = nc.tensor.matmul(ring[:, i % 2], hop2[:, l, k, i * P:(i + 1) * P], x12[:, r, k],
                                                   start=False, stop=(k == NC - 1 and (l, r) == PASSES[-1]))
                    ins.then_inc(hop_full, 1)

            def turn(n, par, before, earlier, earliest, coming, later):
                if before:
                    attention_out(n - 1, 0, earlier)
                if coming:
                    keys(n + 1)
                if before:
                    attention_out(n - 1, 1, earlier)
                if coming:
                    y_chunks(n + 1, before)
                attention(n, par, 0)
                attention(n, par, 1)
                if coming:
                    spread_q(n + 1)
                attention(n, par, 2)
                attention(n, par, 3)
                if before:
                    hops(n - 1, coming)

            pe.wait_ge(wk_ready, 1)
            keys(0)
            y_chunks(0, False)
            spread_q(0)
            pe.wait_ge(hop_ready, 1)
            pe.wait_ge(bias_ready, 3)
            pe.wait_ge(ones_ready, 4)
            turns(pe, turn)
            for c in range(NC):
                attention_out(BATCH - 1, c, True)
            coming.vo_product(pe, 0, stage_v, stage_o, range(NN // 2))
            hops(BATCH - 1, False)
            coming.vo_product(pe, 0, stage_v, stage_o, range(NN // 2, NN))


def kernel_similarity_layers(nc, setup, operands, wlT, wgT, out):
    LAYERS = wlT.shape[0]
    BATCH, C, D = out.shape
    B = operands.BATCHES
    NC, ND = C // P, D // P
    PAIRS = BATCH // B
    ROWS = B * C
    BC = B * NC
    ident, ones_r = setup["ident"], setup["ones_r"]

    with ExitStack() as ctx:
        def sb(name, shape, dt=F32):
            return ctx.enter_context(nc.sbuf_tensor("l_" + name, shape, dt))

        def ps(name, shape):
            return ctx.enter_context(nc.psum_tensor("l_" + name, shape, F32))

        def sem(name):
            return ctx.enter_context(nc.semaphore("l_" + name))

        stage_a, stage_b, x_tr = operands.stage_a, operands.stage_b, operands.x_tr
        adj_off, gate_in, sigma_in = operands.adj_off, operands.gate_in, operands.sigma_in
        consts_loaded, xtr_loaded, z_loaded = operands.consts_loaded, operands.xtr_loaded, operands.z_loaded
        wz2 = operands.wz2
        wvo2 = sb("wvo2", [P, 2, ND, D], F32R)
        small = sb("small", [P, 8])
        spare = sb("spare", [P, 1])
        unread = sb("unread", [P, 2])
        inv_s2 = sb("inv_s2", [P, 1])
        w_l = sb("w_l", [P, 1])
        expo = sb("expo", [P, BC])

        x_res = sb("x_res", [P, BC, D])
        xT2 = sb("xT2", [P, 2, ND, ROWS], F32R)
        z2 = [sb("zl2", [P, 2, ND, ROWS], F32R), sb("zg2", [P, 2, ND, ROWS], F32R)]
        v2 = sb("v2", [P, 2, BC, D], F32R)
        sq = sb("sq", [P, 2, BC])
        sqm = sb("sqm", [P, BC])
        rn = sb("rn", [P, BC])
        gbias = sb("gbias", [P, BC])
        diag = sb("diag", [P, 2, BC, P])
        diag2 = sb("diag2", [P, 2, 2, BC, P], F32R)
        adj_r = sb("adj_r", [P, B, NC, C])
        e_g = sb("e_g", [P, BC, C])
        t_l = sb("t_l", [P, BC, C])
        t_g = sb("t_g", [P, BC, C])
        deg = sb("deg", [P, 2 * BC])
        dm = sb("dm", [P, 2 * BC])
        drec = sb("drec", [P, 2 * BC])
        coef = sb("coef", [P, 2 * BC])
        cnorm = sb("cnorm", [P, 2 * BC])
        km = sb("km", [P, BC, C])
        kT2 = sb("kT2", [P, 2, B, NC, C], F32R)
        s = sb("s", [P, BC, D])
        stats = sb("stats", [P, BC, 6])
        mv = sb("mv", [P, BC, 2])
        ve = sb("ve", [P, BC])
        rstd = sb("rstd", [P, BC])
        nmean = sb("nmean", [P, BC])
        nmr = sb("nmr", [P, BC])

        ring = ps("ring", [P, 2, 512])
        gram = operands.wide[:].rearrange("p (g b) (c f) -> p g b c f", b=B, f=C)
        rbank = ps("rbank", [P, B, C])
        tbank = ps("tbank", [P, NC, C])

        const_step = sem("const_step")
        expo_ready = sem("expo_ready")
        wvo_full = operands.wvo_full
        w_hi, w_lo = operands.w_hi, operands.w_lo
        scalar_exp = sem("scalar_exp")
        scalar_step = sem("scalar_step")
        coef_ready = sem("coef_ready")
        xres_loaded = sem("xres_loaded")
        ring_full = sem("ring_full")
        hi_ready = sem("hi_ready")
        lo_ready = sem("lo_ready")
        gram_full = sem("gram_full")
        diag_ready = sem("diag_ready")
        sqm_ready = sem("sqm_ready")
        rn_ready = sem("rn_ready")
        gbias_ready = sem("gbias_ready")
        dl_ready = sem("dl_ready")
        dhi_ready = sem("dhi_ready")
        dlo_ready = sem("dlo_ready")
        r_full = sem("r_full")
        sq_added = sem("sq_added")
        adjr_ready = sem("adjr_ready")
        tl_ready = sem("tl_ready")
        eg_ready = sem("eg_ready")
        tg_ready = sem("tg_ready")
        coef_step = sem("coef_step")
        ve_ready = sem("ve_ready")
        scaled = sem("scaled")
        k_ready = sem("k_ready")
        kt_full = sem("kt_full")
        kt_hi = sem("kt_hi")
        kt_lo = sem("kt_lo")
        s_ready = sem("s_ready")
        stats_ready = sem("stats_ready")
        mv_ready = sem("mv_ready")
        ln_step = sem("ln_step")
        y_ready = sem("y_ready")
        y_stored = sem("y_stored")

        def pair_rows(pair):
            return pair_chunks(out, pair, B)

        FIRST = ("l0", "l1", "l2", "l3", "g0", "g1", "g2", "g3", "v0", "v1", "v2", "v3")
        FULL = ("t0", "t1", "t2", "t3", "l0", "l1", "l2", "l3", "g0", "g1", "k0", "k1", "g2", "g3", "k2", "k3",
                "v0", "v1", "v2", "v3")
        SHORT = ("k0", "k1", "k2", "k3")

        class Order:

            def __init__(self, names, filled, split):
                self.names, self.filled, self.split = names, filled, split

            def bank(self, name):
                return self.names.index(name) % 2

            def fill(self, name):
                return self.filled + self.names.index(name) + 1

            def splits(self, name):
                return self.split + sum(n[0] != "k" for n in self.names[:self.names.index(name) + 1])

        OPENING = Order(FIRST, ND, ND)

        PRIMED = (y_stored, kt_lo)
        START = 1

        def pairs(engine, turn_of):
            with engine.Fori(0, LAYERS - 1) as layer:
                with engine.Fori(0, PAIRS - 1) as pair:
                    turn_of(layer * PAIRS + pair, FULL)
                turn_of(layer * PAIRS + PAIRS - 1, FULL, layer + 1)
            with engine.Fori((LAYERS - 1) * PAIRS, LAYERS * PAIRS - 1) as u:
                turn_of(u, FULL)
            turn_of(LAYERS * PAIRS - 1, SHORT)

        def turn(u, names):
            return Order(names, ND + len(FIRST) + len(FULL) * u, ND + len(FIRST) + (len(FULL) - BC) * u)

        block = ctx.enter_context(nc.Block())

        @block.sync
        def _(sp):
            sp.wait_ge(lo_ready, ND)
            sp.dma_start(x_tr[:], pair_rows(1)).then_inc(xtr_loaded, 16)

            def load_vo(layer):
                sp.wait_ge(w_lo, 3 * layer + 2)
                operands.load_vo(sp, layer)

            def load_z(layer):
                if layer < LAYERS:
                    sp.wait_ge(wvo_full, layer)
                    sp.dma_start(stage_a[:], weight_chunks(wlT[layer])).then_inc(z_loaded, 16)
                    sp.dma_start(stage_b[:], weight_chunks(wgT[layer])).then_inc(z_loaded, 16)

            sp.wait_ge(w_lo, 2)
            load_z(1)
            for layer in range(LAYERS):
                def step(u, pair, second, turnover=False):
                    sp.wait_ge(y_stored, START + 16 * B * u)
                    sp.dma_start(x_res[:], pair_rows(pair)).then_inc(xres_loaded, 16)
                    if second is not None:
                        sp.wait_ge(lo_ready, turn(u, FULL).splits("t3"))
                        sp.dma_start(x_tr[:], pair_rows(second)).then_inc(xtr_loaded, 16)
                    if turnover:
                        load_vo(layer + 1)
                        load_z(layer + 2)
                    for b in range(B):
                        sp.wait_ge(y_ready, BC * u + NC * (b + 1))
                        sp.dma_start(pair_rows(pair)[:, NC * b:NC * (b + 1)],
                                     s[:, NC * b:NC * (b + 1)]).then_inc(y_stored, 16)

                with sp.Fori(0, PAIRS - 2) as pair:
                    step(layer * PAIRS + pair, pair, pair + 2)
                for pair in (PAIRS - 2, PAIRS - 1):
                    step(layer * PAIRS + pair, pair, pair + 2 - PAIRS if layer < LAYERS - 1 else None,
                         turnover=pair == PAIRS - 1 and layer < LAYERS - 1)
            sp.wait_ge(y_stored, START + 16 * B * LAYERS * PAIRS)
            sp.wait_ge(xtr_loaded, 16 * LAYERS * PAIRS)

        @block.gpsimd
        def _(pool):
            nc.gpsimd.memset(expo[:], -0.5).then_inc(expo_ready, 1)
            pool.wait_ge(expo_ready, 1)
            for i, primed in enumerate(PRIMED):
                nc.gpsimd.memset(unread[:, i:i + 1], 0.0).then_inc(primed, START)
            with pool.Fori(0, LAYERS) as layer:
                with pool.Fori(0, PAIRS) as pair:
                    u = layer * PAIRS + pair

                    pool.wait_ge(sqm_ready, u + 1)
                    nc.gpsimd.tensor_tensor(rn[:], sqm[:], expo[:, 0:BC], ALU.pow).then_inc(rn_ready, 1)
                    for b in range(B):
                        of = slice(NC * b, NC * (b + 1))
                        pool.wait_ge(ve_ready, 2 * (B * u + b) + 2)
                        nc.gpsimd.tensor_tensor(rstd[:, of], ve[:, of], expo[:, of], ALU.pow).then_inc(ln_step, 1)
                        pool.wait_ge(ln_step, 2 * (B * u + b) + 1)
                        nc.gpsimd.tensor_tensor(nmr[:, of], nmean[:, of], rstd[:, of], ALU.mult).then_inc(ln_step, 1)

        @block.scalar
        def _(act):
            def high(order, name):
                dst = {"t": xT2, "l": z2[0], "g": z2[1], "v": v2}[name[0]][:, HI, int(name[1])]
                act.wait_ge(ring_full, order.fill(name))
                nc.scalar.activation(dst, ring[:, order.bank(name)], ACT.Copy).then_inc(hi_ready, 1)


            def layer_scalars(layer):
                act.wait_ge(scalar_step, 6 * layer + 2)
                nc.scalar.activation(small[:, 2:3], small[:, 0:1], ACT.Exp, scale=-1.0).then_inc(scalar_exp, 1)
                nc.scalar.activation(inv_s2[:], small[:, 1:2], ACT.Exp, scale=-2.0).then_inc(scalar_exp, 1)

            def vo_weights(layer):
                act.wait_ge(wvo_full, layer + 1)
                nc.scalar.activation(wvo2[:, HI], operands.wide[:],
                                     ACT.Copy).then_inc(w_hi, 1)

            for t in range(ND):
                high(Order(FULL, 0, 0), f"t{t}")
            layer_scalars(0)
            vo_weights(0)
            for name in FIRST:
                high(OPENING, name)

            def turn_of(u, names, new_layer=None):
                order = turn(u, names)

                def coming(*wanted):
                    for name in wanted:
                        if name in names:
                            high(order, name)

                def exps(b):
                    act.wait_ge(sq_added, B * u + b + 1)
                    act.wait_ge(gbias_ready, B * u + b + 1)
                    for c in range(NC):
                        i = NC * b + c
                        nc.scalar.activation(e_g[:, i], gram[:, 1, b, c], ACT.Exp, bias=gbias[:, i:i + 1],
                                             scale=inv_s2[:]).then_inc(eg_ready, 1)

                def kt_high(b):
                    act.wait_ge(kt_full, B * u + b + 1)
                    nc.scalar.activation(kT2[:, HI, b], tbank[:], ACT.Copy).then_inc(kt_hi, 1)

                def normalise(b):
                    act.wait_ge(ln_step, 2 * (B * u + b) + 2)
                    for i in range(NC * b, NC * (b + 1)):
                        nc.scalar.activation(s[:, i], s[:, i], ACT.Identity, bias=nmr[:, i:i + 1],
                                             scale=rstd[:, i:i + 1]).then_inc(y_ready, 1)

                if new_layer is not None:
                    for i in range(2):
                        operands.weight_high(act, new_layer, i)
                coming("t0", "t1", "t2", "t3", "l0")
                exps(0)
                exps(1)
                coming("l1", "l2", "l3", "g0")
                kt_high(0)
                coming("g1")
                kt_high(1)
                if new_layer is not None:
                    vo_weights(new_layer)
                coming("g2", "g3")
                normalise(0)
                coming("v0", "v1")
                normalise(1)
                coming("v2", "v3")
                if new_layer is not None:
                    layer_scalars(new_layer)

            pairs(act, turn_of)

        @block.vector
        def _(dve):
            steps = [0]

            def step(ins):
                steps[0] += 1
                ins.then_inc(const_step, 1)
                dve.wait_ge(const_step, steps[0])

            def low(order, name):
                buf, i = {"t": xT2, "l": z2[0], "g": z2[1], "v": v2}[name[0]], int(name[1])
                dve.wait_ge(hi_ready, order.splits(name))
                nc.vector.tensor_tensor(buf[:, LO, i], ring[:, order.bank(name)], buf[:, HI, i].bitcast(F32),
                                        ALU.subtract).then_inc(lo_ready, 1)


            def layer_scalars(layer):
                def scalar(ins, n):
                    ins.then_inc(scalar_step, 1)
                    dve.wait_ge(scalar_step, 6 * layer + n)

                scalar(nc.vector.tensor_copy(small[:, 0:1], gate_in[:, bass.ds(layer, 1)]), 1)
                scalar(nc.vector.tensor_copy(small[:, 1:2], sigma_in[:, bass.ds(layer, 1)]), 2)
                dve.wait_ge(scalar_exp, 2 * layer + 1)
                scalar(nc.vector.tensor_scalar(small[:, 3:4], small[:, 2:3], 1.0, None, ALU.add), 3)
                scalar(nc.vector.reciprocal(w_l[:], small[:, 3:4]), 4)
                scalar(nc.vector.tensor_scalar(small[:, 4:5], w_l[:], -1.0, 1.0, ALU.mult, ALU.add), 5)
                dve.wait_ge(expo_ready, 1)
                scalar(nc.vector.tensor_scalar(coef[:, BC:2 * BC], expo[:, 0:BC], 0.0, small[:, 4:5],
                                               ALU.mult, ALU.add), 6)
                dve.wait_ge(scalar_exp, 2 * layer + 2)
                nc.vector.tensor_copy(small[:, 5:6], inv_s2[:]).then_inc(coef_ready, 1)

            def vo_weights(layer):
                dve.wait_ge(w_hi, 3 * layer + 3)
                nc.vector.tensor_tensor(wvo2[:, LO], operands.wide[:],
                                        wvo2[:, HI].bitcast(F32), ALU.subtract).then_inc(w_lo, 1)

            for t in range(ND):
                low(Order(FULL, 0, 0), f"t{t}")
            dve.wait_ge(consts_loaded, 48)
            layer_scalars(0)
            for c in range(NC):
                block_ = adj_off[:, c, c * P:(c + 1) * P]
                step(nc.vector.tensor_tensor(diag[:, 0, c], block_, ident[:], ALU.mult))
                step(nc.vector.tensor_tensor(block_, block_, diag[:, 0, c], ALU.subtract))
            vo_weights(0)
            for name in FIRST:
                low(OPENING, name)

            def turn_of(u, names, new_layer=None):
                order = turn(u, names)

                def coming(*wanted):
                    for name in wanted:
                        if name in names:
                            low(order, name)

                def diagonals(g, b):
                    dve.wait_ge(gram_full, 2 * B * u + B * g + b + 1)
                    for c in range(NC):
                        i = NC * b + c
                        nc.vector.tensor_tensor_reduce(
                            out=diag[:, g, i], in0=gram[:, g, b, c, c * P:(c + 1) * P], in1=ident[:],
                            scale=(1.0, -0.5)[g], scalar=0.0, op0=ALU.mult, op1=ALU.add,
                            accum_out=sq[:, g, i:i + 1]).then_inc(diag_ready, 1)

                def gaussian_bias(b):
                    of = slice(NC * b, NC * (b + 1))
                    dve.wait_ge(diag_ready, 2 * BC * u + BC + NC * (b + 1))
                    nc.vector.tensor_scalar(gbias[:, of], sq[:, 1, of], inv_s2[:], None,
                                            ALU.mult).then_inc(gbias_ready, 1)

                def coefs(ins, n):
                    ins.then_inc(coef_step, 1)
                    dve.wait_ge(coef_step, 5 * u + n)

                def split_diag(g, of, nth, ready, count):
                    dve.wait_ge(ready, count)
                    nc.vector.tensor_copy(diag2[:, g, HI, of], diag[:, g, of]).then_inc(dhi_ready, 1)
                    dve.wait_ge(dhi_ready, (B + 1) * u + nth)
                    nc.vector.tensor_tensor(diag2[:, g, LO, of], diag[:, g, of],
                                            diag2[:, g, HI, of].bitcast(F32), ALU.subtract).then_inc(dlo_ready, 1)

                def cosines(b):
                    dve.wait_ge(r_full, u + 1)
                    for c in range(NC):
                        nc.vector.tensor_tensor(adj_r[:, b, c], rbank[:, b], adj_off[:, c],
                                                ALU.mult).then_inc(adjr_ready, 1)
                    for c in range(NC):
                        i = NC * b + c
                        dve.wait_ge(adjr_ready, BC * u + i + 1)
                        nc.vector.scalar_tensor_tensor(
                            out=t_l[:, i], in0=gram[:, 0, b, c], scalar=0.0, in1=adj_r[:, b, c],
                            op0=ALU.max, op1=ALU.mult, accum_out=deg[:, i:i + 1]).then_inc(tl_ready, 1)

                def gaussians(b):
                    for c in range(NC):
                        i = NC * b + c
                        dve.wait_ge(eg_ready, BC * u + i + 1)
                        nc.vector.scalar_tensor_tensor(
                            out=t_g[:, i], in0=e_g[:, i], scalar=1.0, in1=adj_off[:, c],
                            op0=ALU.min, op1=ALU.mult, accum_out=deg[:, BC + i:BC + i + 1]).then_inc(tg_ready, 1)

                def combine(b):
                    for i in range(NC * b, NC * (b + 1)):
                        nc.vector.tensor_scalar(t_g[:, i], t_g[:, i], cnorm[:, BC + i:BC + i + 1], None,
                                                ALU.mult).then_inc(scaled, 1)
                    for i in range(NC * b, NC * (b + 1)):
                        dve.wait_ge(scaled, BC * u + i + 1)
                        nc.vector.scalar_tensor_tensor(out=km[:, i], in0=t_l[:, i], scalar=cnorm[:, i:i + 1],
                                                       in1=t_g[:, i], op0=ALU.mult, op1=ALU.add).then_inc(k_ready, 1)

                def kt_low(b):
                    dve.wait_ge(kt_hi, B * u + b + 1)
                    nc.vector.tensor_tensor(kT2[:, LO, b], tbank[:], kT2[:, HI, b].bitcast(F32),
                                            ALU.subtract).then_inc(kt_lo, 1)

                def residual(i):
                    dve.wait_ge(ring_full, order.fill(f"k{i}"))
                    if i == 0:
                        dve.wait_ge(xres_loaded, 16 * u + 16)
                    if i % NC == 0:
                        dve.wait_ge(y_stored, START + 16 * B * u)
                    nc.vector.tensor_tensor(s[:, i], ring[:, order.bank(f"k{i}")], x_res[:, i],
                                            ALU.add).then_inc(s_ready, 1)

                def row_stats(i):
                    dve.wait_ge(s_ready, BC * u + i + 1)
                    nc.vector.bn_stats(stats[:, i], s[:, i]).then_inc(stats_ready, 1)

                def row_moments(b):
                    of = slice(NC * b, NC * (b + 1))
                    dve.wait_ge(stats_ready, BC * u + NC * (b + 1))
                    nc.vector.memset(spare[:], 0.0)
                    for i in range(NC * b, NC * (b + 1)):
                        nc.vector.bn_aggr(mv[:, i], stats[:, i]).then_inc(mv_ready, 1)
                    dve.wait_ge(mv_ready, BC * u + NC * (b + 1))
                    nc.vector.tensor_scalar(ve[:, of], mv[:, of, 1], LN_EPS, None, ALU.add).then_inc(ve_ready, 1)
                    nc.vector.tensor_scalar(nmean[:, of], mv[:, of, 0], -1.0, None, ALU.mult).then_inc(ve_ready, 1)

                if new_layer is not None:
                    for i in range(2):
                        operands.weight_low(dve, new_layer, i)
                diagonals(0, 0)
                coming("t0")
                diagonals(0, 1)
                dve.wait_ge(diag_ready, 2 * BC * u + BC)
                nc.vector.tensor_scalar(sqm[:], sq[:, 0], DEG_EPS * DEG_EPS, None, ALU.max).then_inc(sqm_ready, 1)
                coming("t1", "t2")
                diagonals(1, 0)
                gaussian_bias(0)
                coming("t3")
                split_diag(1, slice(0, NC), 1, diag_ready, 2 * BC * u + BC + NC)
                dve.wait_ge(rn_ready, u + 1)
                for i in range(BC):
                    nc.vector.tensor_scalar(diag[:, 0, i], ident[:], rn[:, i:i + 1], None,
                                            ALU.mult).then_inc(dl_ready, 1)
                split_diag(0, slice(0, BC), 2, dl_ready, BC * u + BC)
                coefs(nc.vector.tensor_scalar(coef[:, 0:BC], rn[:], w_l[:], None, ALU.mult), 1)
                diagonals(1, 1)
                gaussian_bias(1)
                split_diag(1, slice(NC, BC), 3, diag_ready, 2 * BC * u + 2 * BC)
                coming("l0")
                cosines(0)
                coming("l1")
                cosines(1)
                gaussians(0)
                coming("l2")
                gaussians(1)
                dve.wait_ge(tl_ready, BC * u + BC)
                coefs(nc.vector.tensor_tensor(deg[:, 0:BC], deg[:, 0:BC], rn[:], ALU.mult), 2)
                dve.wait_ge(tg_ready, BC * u + BC)
                coefs(nc.vector.tensor_scalar(dm[:], deg[:], DEG_EPS, None, ALU.max), 3)
                coefs(nc.vector.reciprocal(drec[:], dm[:]), 4)
                coefs(nc.vector.tensor_tensor(cnorm[:], drec[:], coef[:], ALU.mult), 5)
                combine(0)
                coming("l3")
                combine(1)
                coming("g0")
                kt_low(0)
                coming("g1")
                residual(0)
                row_stats(0)
                kt_low(1)
                residual(1)
                row_stats(1)
                if new_layer is not None:
                    vo_weights(new_layer)
                coming("g2")
                row_moments(0)
                coming("g3")
                residual(2)
                row_stats(2)
                residual(3)
                row_stats(3)
                row_moments(1)
                coming("v0", "v1", "v2", "v3")
                if new_layer is not None:
                    layer_scalars(new_layer)

            pairs(dve, turn_of)

        @block.tensor
        def _(pe):
            def product(bank, lhs, rhs, ks, sem, start=True):
                n = 0
                for k in ks:
                    for l, r in PASSES:
                        ins = nc.tensor.matmul(bank, lhs(l, k), rhs(r, k), start=(start and n == 0),
                                               stop=(n == 3 * len(ks) - 1), skip_group_check=not start)
                        n += 1
                ins.then_inc(sem, 1)

            def transpose_x(t, bank):
                for i in range(BC):
                    ins = nc.tensor.transpose(ring[:, bank, i * P:(i + 1) * P], x_tr[:, i, t * P:(t + 1) * P], ident[:])
                ins.then_inc(ring_full, 1)

            def weighted(w, names, before):
                for name in names:
                    bank, i = before(name), int(name[1])
                    if name[0] == "v":
                        product(bank, lambda h, k: xT2[:, h, k, i * P:(i + 1) * P],
                                lambda h, k: w[:, h, k], range(ND), ring_full)
                    else:
                        product(bank, lambda h, k: w[:, h, k, i * P:(i + 1) * P],
                                lambda h, k: xT2[:, h, k], range(ND), ring_full)

            pe.wait_ge(xtr_loaded, 16)
            for t in range(ND):
                if t >= 2:
                    pe.wait_ge(lo_ready, t - 1)
                transpose_x(t, t % 2)

            def opened(name):
                n = FIRST.index(name)
                if n >= 2:
                    pe.wait_ge(lo_ready, OPENING.splits(FIRST[n - 2]))
                return ring[:, OPENING.bank(name)]

            pe.wait_ge(lo_ready, ND)
            pe.wait_ge(w_lo, 1)
            weighted(wz2[0], FIRST[0:ND], opened)
            pe.wait_ge(w_lo, 2)
            weighted(wz2[1], FIRST[ND:2 * ND], opened)
            pe.wait_ge(w_lo, 3)
            weighted(wvo2, FIRST[2 * ND:], opened)

            def turn_of(u, names, new_layer=None):
                order = turn(u, names)

                def free(name):
                    n = names.index(name)
                    if n < 2:
                        pe.wait_ge(lo_ready, order.split + n - 1)
                    elif names[n - 2][0] == "k":
                        pe.wait_ge(s_ready, BC * u + int(names[n - 2][1]) + 1)
                    else:
                        pe.wait_ge(lo_ready, order.splits(names[n - 2]))
                    return ring[:, order.bank(name)]

                def coming(w, *wanted):
                    weighted(w, [name for name in wanted if name in names], free)

                def grams(g, b):
                    if b == 0:
                        pe.wait_ge(lo_ready, order.split - (2 - g) * ND)
                    n = 0
                    for c in range(NC):
                        rows = slice(b * C + c * P, b * C + (c + 1) * P)
                        for k in range(ND):
                            for l, r in PASSES:
                                ins = nc.tensor.matmul(
                                    gram[:, g, b, c], z2[g][:, l, k, rows], z2[g][:, r, k, b * C:(b + 1) * C],
                                    start=(n == 0), stop=(n == 2 * 3 * ND - 1), skip_group_check=True)
                                n += 1
                    ins.then_inc(gram_full, 1)

                def x_chunk(t):
                    if f"t{t}" not in names:
                        return
                    if t == 0:
                        pe.wait_ge(xtr_loaded, 16 * u + 32)
                    free(f"t{t}")
                    transpose_x(t, order.bank(f"t{t}"))

                def column_norms():
                    pe.wait_ge(dlo_ready, (B + 1) * u + 2)
                    for h in (HI, LO):
                        ins = nc.tensor.matmul(rbank[:].rearrange("p b f -> p (b f)"), ones_r[:],
                                               diag2[:, 0, h].rearrange("p i f -> p (i f)"),
                                               start=(h == HI), stop=(h == LO))
                    ins.then_inc(r_full, 1)

                def add_squares(b):
                    pe.wait_ge(dlo_ready, (B + 1) * u + (1, 3)[b])
                    for c in range(NC):
                        for h in (HI, LO):
                            ins = nc.tensor.matmul(
                                gram[:, 1, b, c], ones_r[:],
                                diag2[:, 1, h, NC * b:NC * (b + 1)].rearrange("p i f -> p (i f)"),
                                start=False, stop=(c == NC - 1 and h == LO), skip_group_check=True)
                    ins.then_inc(sq_added, 1)

                def transposed_k(b):
                    pe.wait_ge(k_ready, BC * u + NC * (b + 1))
                    pe.wait_ge(kt_lo, START + B * u + b)
                    for m in range(NC):
                        for c in range(NC):
                            ins = nc.tensor.transpose(tbank[:, m, c * P:(c + 1) * P],
                                                      km[:, NC * b + c, m * P:(m + 1) * P], ident[:])
                    ins.then_inc(kt_full, 1)

                def kv(i):
                    b, c = i // NC, i % NC
                    pe.wait_ge(kt_lo, START + B * u + b + 1)
                    product(free(f"k{i}"), lambda h, m: kT2[:, h, b, m, c * P:(c + 1) * P],
                            lambda h, m: v2[:, h, NC * b + m], range(NC), ring_full)

                grams(0, 0)
                x_chunk(0)
                grams(0, 1)
                x_chunk(1)
                x_chunk(2)
                grams(1, 0)
                x_chunk(3)
                grams(1, 1)
                if "l0" in names:
                    pe.wait_ge(lo_ready, order.splits("t3"))
                if new_layer is not None:
                    pe.wait_ge(w_lo, 3 * new_layer + 1)
                coming(wz2[0], "l0")
                column_norms()
                add_squares(0)
                add_squares(1)
                coming(wz2[0], "l1", "l2", "l3")
                if new_layer is not None:
                    pe.wait_ge(w_lo, 3 * new_layer + 2)
                coming(wz2[1], "g0")
                transposed_k(0)
                coming(wz2[1], "g1")
                kv(0)
                transposed_k(1)
                kv(1)
                if new_layer is not None:
                    operands.vo_product(pe, new_layer, [stage_a[:, f] for f in range(ND)],
                                    [stage_b[:, f] for f in range(ND)], range(ND))
                coming(wz2[1], "g2", "g3")
                kv(2)
                kv(3)
                if new_layer is not None:
                    pe.wait_ge(w_lo, 3 * new_layer + 3)
                coming(wvo2, "v0", "v1", "v2", "v3")

            pairs(pe, turn_of)


def build(nc, x, adj, adjT, columns, bm, bias, wlT, wgT, wv, woT, gate, log_sigma, out):
    with ExitStack() as ctx:
        ident = ctx.enter_context(nc.sbuf_tensor("ident", [P, P], F32))
        ones = ctx.enter_context(nc.sbuf_tensor("ones", [P, P], F32))
        ones_r = ctx.enter_context(nc.sbuf_tensor("ones_r", [P, P], F32R))
        ident_zero = ctx.enter_context(nc.semaphore("ident_zero"))
        ones_done = ctx.enter_context(nc.semaphore("ones_done"))
        with nc.Block() as block:
            @block.gpsimd
            def _(pool):
                nc.gpsimd.memset(ident[:], 0.0).then_inc(ident_zero, 1)
                pool.wait_ge(ident_zero, 1)
                nc.gpsimd.affine_select(out=ident[:], in_=ident[:], compare_op=ALU.not_equal, fill=1.0, base=0,
                                        pattern=[[-1, P]], channel_multiplier=1)

            @block.vector
            def _(dve):
                nc.vector.memset(ones[:], 1.0).then_inc(ones_done, 1)
                dve.wait_ge(ones_done, 1)
                nc.vector.tensor_copy(ones_r[:], ones[:])

        setup = {"ident": ident, "ones": ones, "ones_r": ones_r}
        operands = LayerOperands(nc, ctx, out, adj, wlT, wgT, wv, woT, gate, log_sigma)
        attention_and_hop(nc, setup, x, adj, adjT, columns, bm, bias, out, operands)
        kernel_similarity_layers(nc, setup, operands, wlT, wgT, out)


def kernel(**inputs):
    import numpy as np
    import concourse.bacc as bacc
    from concourse.bass_utils import run_bass_kernel_spmd as run

    def layers(name, turn):
        both = [np.asarray(inputs[f"L{i}_gnn_{name}"]) for i in (2, 3)]
        return np.ascontiguousarray(np.stack([w.T if turn else w for w in both]))

    def columns(*names):
        return np.ascontiguousarray(np.stack([np.asarray(inputs[n]).reshape(-1, P).T for n in names], axis=1))

    arrays = {
        "x": np.asarray(inputs["x"]),
        "adj": np.asarray(inputs["adj"]),
        "adjT": np.ascontiguousarray(np.asarray(inputs["adj"]).T),
        "columns": columns("L0_gnn_wq", "L0_gnn_wk"),
        "bm": np.asarray(inputs["L0_gnn_bm"]),
        "bias": np.asarray(inputs["L1_gnn_bias"]),
        "wlT": layers("W_lang", True),
        "wgT": layers("W_grav", True),
        "wv": layers("W_V", False),
        "woT": layers("W_O", True),
        "gate": layers("gate_logit", False),
        "log_sigma": layers("log_sigma", False),
    }
    nc = bacc.Bacc("TRN2", target_bir_lowering=False, num_devices=1)
    args = [nc.dram_tensor(f"in_{k}", a.shape, mybir.dt.from_np(a.dtype), kind="ExternalInput").ap()
            for k, a in arrays.items()]
    out = nc.dram_tensor("out_x", arrays["x"].shape, F32, kind="ExternalOutput").ap()
    build(nc, *args, out)
    r = run(nc, [{f"in_{k}": a for k, a in arrays.items()}], core_ids=[0])
    return r.results[0]["out_x"]
```
